# Optimizing a Trainium2 kernel written in Bass

```python
import numpy as np
import jax
import jax.numpy as jnp

def _softmax(x, axis=-1):
    return jax.nn.softmax(x, axis=axis)

def _gelu(x):
    return jax.nn.gelu(x, approximate=True)

def _silu(x):
    return jax.nn.silu(x)

def _sigmoid(x):
    return jax.nn.sigmoid(x)

def _layernorm(x, axis=-1, eps=1e-05):
    m = jnp.mean(x, axis=axis, keepdims=True)
    v = jnp.var(x, axis=axis, keepdims=True)
    return (x - m) / jnp.sqrt(v + eps)

def _scatter_add(tgt, idx, src, axis=0):
    return tgt.at[idx].add(src)

def _segment_sum(src, seg, n):
    return jax.ops.segment_sum(src, seg, n)
kernel_name = 'mk_macaron_d1_jaxref_r8_bb712d'

def setup_inputs(seed: int=0):
    np.random.seed(seed)
    _w = jnp.asarray

    def _L0_attn_setup():
        import jax, jax.numpy as jnp
        import numpy as np
        import math
        D_MODEL = 128
        NUM_HEADS = 16
        B, L = (2, 256)
        PERIODS = (1.0, 30.0)
        WEIGHTS = (0.8, 0.4)
        SIGMAS = (0.5, 2.0)

        def _gaussian_mask(length):
            idx = jnp.arange(length, dtype=jnp.float32)
            delta = jnp.abs(idx[:, None] - idx[None, :])
            mask = jnp.zeros_like(delta)
            for p, w, sigma in zip(PERIODS, WEIGHTS, SIGMAS):
                if p < 0.2:
                    continue
                mask = mask + w * jnp.exp(-(delta - p) ** 2 / (2.0 * sigma ** 2))
            return mask
        key = jax.random.key(seed)
        ks = jax.random.split(key, 10)
        s = 1.0 / math.sqrt(D_MODEL)
        inp = {'x': jax.random.normal(ks[0], (B, L, D_MODEL), dtype=jnp.float32), 'Wq': jax.random.normal(ks[1], (D_MODEL, D_MODEL), dtype=jnp.float32) * s, 'bq': jax.random.normal(ks[2], (D_MODEL,), dtype=jnp.float32) * 0.01, 'Wk': jax.random.normal(ks[3], (D_MODEL, D_MODEL), dtype=jnp.float32) * s, 'bk': jax.random.normal(ks[4], (D_MODEL,), dtype=jnp.float32) * 0.01, 'Wv': jax.random.normal(ks[5], (D_MODEL, D_MODEL), dtype=jnp.float32) * s, 'bv': jax.random.normal(ks[6], (D_MODEL,), dtype=jnp.float32) * 0.01, 'Wo': jax.random.normal(ks[7], (D_MODEL, D_MODEL), dtype=jnp.float32) * s, 'bo': jax.random.normal(ks[8], (D_MODEL,), dtype=jnp.float32) * 0.01, 'prior_lambda': jnp.asarray(2.0, dtype=jnp.float32)}
        return inp
    _L0_attn_in = _L0_attn_setup()

    def _L0_ffn_setup():
        import jax, jax.numpy as jnp
        import numpy as np
        B, S, D = (2, 256, 128)
        DFF = 256
        E_FFN = 8
        E_ZERO = 4
        E_TOT = E_FFN + E_ZERO
        TOP_K = 2
        key = jax.random.key(seed)
        k1, k2, k3, k4 = jax.random.split(key, 4)
        x = jax.random.normal(k1, (B, S, D), dtype=jnp.float32)
        gate_w = jax.random.normal(k2, (E_TOT, D), dtype=jnp.float32) * (1.0 / np.sqrt(D))
        expert_bias = jnp.zeros((E_TOT,), dtype=jnp.float32)
        w1 = jax.random.normal(k3, (E_FFN, DFF, D), dtype=jnp.float32) * (1.0 / np.sqrt(D))
        w2 = jax.random.normal(k4, (E_FFN, D, DFF), dtype=jnp.float32) * (1.0 / np.sqrt(DFF))
        return {'x': x, 'gate_w': gate_w, 'expert_bias': expert_bias, 'w1': w1, 'w2': w2}
    _L0_ffn_in = _L0_ffn_setup()
    _d = {'L0_attn_x': _L0_attn_in['x'], 'L0_attn_Wq': _L0_attn_in['Wq'], 'L0_attn_bq': _L0_attn_in['bq'], 'L0_attn_Wk': _L0_attn_in['Wk'], 'L0_attn_bk': _L0_attn_in['bk'], 'L0_attn_Wv': _L0_attn_in['Wv'], 'L0_attn_bv': _L0_attn_in['bv'], 'L0_attn_Wo': _L0_attn_in['Wo'], 'L0_attn_bo': _L0_attn_in['bo'], 'L0_attn_prior_lambda': _L0_attn_in['prior_lambda'], 'L0_ffn_gate_w': _L0_ffn_in['gate_w'], 'L0_ffn_expert_bias': _L0_ffn_in['expert_bias'], 'L0_ffn_w1': _L0_ffn_in['w1'], 'L0_ffn_w2': _L0_ffn_in['w2']}
    _x0 = _d['L0_attn_x']
    _d['L0_attn_x'] = jax.random.normal(jax.random.fold_in(jax.random.key(seed), 1), (32, 256, 128), dtype=_x0.dtype)
    del _x0
    return _d

def reference(L0_attn_x, L0_attn_Wq, L0_attn_bq, L0_attn_Wk, L0_attn_bk, L0_attn_Wv, L0_attn_bv, L0_attn_Wo, L0_attn_bo, L0_attn_prior_lambda, L0_ffn_gate_w, L0_ffn_expert_bias, L0_ffn_w1, L0_ffn_w2):

    def _L0_attn_ref(x, Wq, bq, Wk, bk, Wv, bv, Wo, bo, prior_lambda):
        import jax, jax.numpy as jnp
        import numpy as np
        import math
        D_MODEL = 128
        NUM_HEADS = 16
        B, L = (2, 256)
        PERIODS = (1.0, 30.0)
        WEIGHTS = (0.8, 0.4)
        SIGMAS = (0.5, 2.0)

        def _gaussian_mask(length):
            idx = jnp.arange(length, dtype=jnp.float32)
            delta = jnp.abs(idx[:, None] - idx[None, :])
            mask = jnp.zeros_like(delta)
            for p, w, sigma in zip(PERIODS, WEIGHTS, SIGMAS):
                if p < 0.2:
                    continue
                mask = mask + w * jnp.exp(-(delta - p) ** 2 / (2.0 * sigma ** 2))
            return mask
        Bx, Lx, D = x.shape
        H = NUM_HEADS
        hd = D // H

        def split_heads(t):
            return t.reshape(Bx, Lx, H, hd).transpose(0, 2, 1, 3)
        Q = split_heads(x @ Wq.T + bq)
        K = split_heads(x @ Wk.T + bk)
        V = split_heads(x @ Wv.T + bv)
        scores = jnp.einsum('bhqd,bhkd->bhqk', Q, K) / math.sqrt(hd)
        scores = scores + prior_lambda * _gaussian_mask(Lx)[None, None, :, :]
        attn = jax.nn.softmax(scores, axis=-1)
        out = jnp.einsum('bhqk,bhkd->bhqd', attn, V)
        out = out.transpose(0, 2, 1, 3).reshape(Bx, Lx, D)
        return out @ Wo.T + bo

    def _L0_ffn_ref(x, gate_w, expert_bias, w1, w2):
        import jax, jax.numpy as jnp
        import numpy as np
        B, S, D = (2, 256, 128)
        DFF = 256
        E_FFN = 8
        E_ZERO = 4
        E_TOT = E_FFN + E_ZERO
        TOP_K = 2
        logits = jnp.einsum('btd,ed->bte', x, gate_w) + expert_bias
        topk_logits, topk_idx = jax.lax.top_k(logits, TOP_K)
        topk_w = jax.nn.softmax(topk_logits, axis=-1)
        onehot = jax.nn.one_hot(topk_idx, E_TOT, dtype=x.dtype)
        w = jnp.einsum('btk,btke->bte', topk_w, onehot)
        w_ffn = w[..., :E_FFN]
        w_zero = jnp.sum(w[..., E_FFN:], axis=-1)
        h = jax.nn.silu(jnp.einsum('btd,efd->btef', x, w1))
        y = jnp.einsum('btef,edf->bted', h, w2)
        out = jnp.einsum('bte,bted->btd', w_ffn, y) + w_zero[..., None] * x
        return out
    x = L0_attn_x
    x = x + 0.5 * _L0_ffn_ref(_layernorm(x, axis=-1), L0_ffn_gate_w, L0_ffn_expert_bias, L0_ffn_w1, L0_ffn_w2)
    x = x + _L0_attn_ref(_layernorm(x, axis=-1), L0_attn_Wq, L0_attn_bq, L0_attn_Wk, L0_attn_bk, L0_attn_Wv, L0_attn_bv, L0_attn_Wo, L0_attn_bo, L0_attn_prior_lambda)
    x = x + 0.5 * _L0_ffn_ref(_layernorm(x, axis=-1), L0_ffn_gate_w, L0_ffn_expert_bias, L0_ffn_w1, L0_ffn_w2)
    return x

_drawn_inputs = setup_inputs


def setup_inputs(seed=0):
    import zlib

    import numpy as np

    out = dict(_drawn_inputs(seed))
    spreads = {'L0_ffn_expert_bias': (0.0, 0.1)}
    factors = {'L0_attn_bq': 28.316, 'L0_attn_bk': 64.0, 'L0_attn_bv': 3.833, 'L0_attn_bo': 3.742}
    for name, (base, spread) in spreads.items():
        noise = np.random.default_rng([zlib.crc32(name.encode()), seed]).standard_normal(out[name].shape)
        drawn = base * np.exp(spread * noise) if base else spread * noise
        out[name] = jnp.asarray(drawn.astype(out[name].dtype))
    for name, factor in factors.items():
        out[name] = (out[name] * factor).astype(out[name].dtype)
    return out
```

```python
from contextlib import ExitStack

import concourse.bass as bass
from concourse import mybir

F32 = mybir.dt.float32
F32R = mybir.dt.float32r
BF16 = mybir.dt.bfloat16
ALU = mybir.AluOpType
ACT = mybir.ActivationFunctionType
AX = mybir.AxisListType

P = 128


def wait(eng, sem, value):
    if not (isinstance(value, int) and value <= 0):
        eng.wait_ge(sem, value)


def alone(eng, waits_met):
    eng.sem_inc(waits_met, 1)


def bc(ap, axis, n):
    ap = ap.unsqueeze(axis)
    shape = list(ap.shape)
    shape[axis] = n
    return ap.broadcast_to(shape)


def build(nc, x, wq, bq, wk, bk, wv, bv, wo, bo, lam, gate, ebias, w1, w2, ident, prior, out):
    N, D = x.shape
    E = gate.shape[1]
    FE = w1.shape[1] // 256
    L = prior.shape[0]
    H, HD = 16, 8
    TILES = N // P
    BT = 4
    BLK = BT * P
    NB = TILES // BT
    NBATCH = N // L
    SPARE = BT
    G, J = 4, 4
    KT = L // P
    QSCALE = float(HD) ** -0.5
    EPS = 1e-5
    LOWEST = -3.0e38
    assert D == P and FE * 256 == w1.shape[1] and KT == 2 and G * J == H and E == 12

    with ExitStack() as ctx:
        def sb(name, shape, dt=F32):
            return ctx.enter_context(nc.sbuf_tensor(name, shape, dt))

        def sem(name):
            return ctx.enter_context(nc.semaphore(name))

        x_all = sb("x_all", [P, (TILES + SPARE) * D])
        w1_f = sb("w1_f", [P, FE * 256])
        w2_f = sb("w2_f", [P, FE * 2 * D])
        w1_hi = sb("w1_hi", [P, FE * 2, P], BF16)
        w1_lo = sb("w1_lo", [P, FE * 2, P], BF16)
        w2_hi = sb("w2_hi", [P, FE * 2, D], BF16)
        w2_lo = sb("w2_lo", [P, FE * 2, D], BF16)
        gate_t = sb("gate_t", [P, E])
        ebias_b = sb("ebias_b", [P, E])
        ident_f = sb("ident_f", [P, P])
        ident_r = sb("ident_r", [P, P], F32R)
        ident_h = sb("ident_h", [P, P], BF16)
        rank = sb("rank", [P, E])
        neg_half = sb("neg_half", [P, BT])

        stats = sb("stats", [P, BT, 6])
        meanvar = sb("meanvar", [P, BT, 2])
        var_eps = sb("var_eps", [P, BT])
        rstd = sb("rstd", [P, BT])
        xn = sb("xn", [P, BT, D])
        xt_f = sb("xt_f", [P, BLK])
        xt_hi = sb("xt_hi", [P, BLK], BF16)
        xt_lo = sb("xt_lo", [P, BLK], BF16)
        h_f = sb("h_f", [P, 2, 2, BLK])
        h_hi = sb("h_hi", [P, 2, 2, BLK], BF16)
        h_lo = sb("h_lo", [P, 2, 2, BLK], BF16)
        logits = sb("logits", [P, BT, E])
        masked = sb("masked", [P, BT, E])
        eq = sb("eq", [P, BT, E])
        ranked = sb("ranked", [P, BT, E])
        first = sb("first", [P, BT])
        top0 = sb("top0", [P, BT])
        top1 = sb("top1", [P, BT])
        hot0 = sb("hot0", [P, BT, E])
        hot1 = sb("hot1", [P, BT, E])
        gap = sb("gap", [P, BT])
        tanh_gap = sb("tanh_gap", [P, BT])
        half_w0 = sb("half_w0", [P, BT])
        half_w1 = sb("half_w1", [P, BT])
        part0 = sb("part0", [P, BT, E])
        part1 = sb("part1", [P, BT, E])
        w_tok = sb("w_tok", [P, BT, E])
        w_zero = sb("w_zero", [P, BT])

        wstage = sb("wstage", [P, 4, P])
        wq_s = sb("wq_s", [P, P])
        wq_hi = sb("wq_hi", [P, H, 32], BF16)
        wq_lo = sb("wq_lo", [P, H, 32], BF16)
        wk_hi = sb("wk_hi", [P, H, 32], BF16)
        wk_lo = sb("wk_lo", [P, H, 32], BF16)
        wv_hi = sb("wv_hi", [P, P], BF16)
        wv_lo = sb("wv_lo", [P, P], BF16)
        wo_hi = sb("wo_hi", [P, P], BF16)
        wo_lo = sb("wo_lo", [P, P], BF16)
        bstage = sb("bstage", [1, 2, P])
        bias_f = sb("bias_f", [1, 2, H, 32])
        bias_r = sb("bias_r", [1, 2, H, 32])
        bias_p = sb("bias_p", [1, 3, 2, H, 32], BF16)
        bias_rows = sb("bias_rows", [3, 2, H, 32], BF16)
        ones_row = sb("ones_row", [3, L], BF16)
        neg_lo = sb("neg_lo", [P, 2])
        bv_b = sb("bv_b", [P, D])
        bo_b = sb("bo_b", [P, D])
        lam_b = sb("lam_b", [P, 1])
        prior_f = sb("prior_f", [P, KT, L])
        prior_hi = sb("prior_hi", [P, KT, L], F32R)
        prior_lo = sb("prior_lo", [P, KT, L], F32R)

        a_stats = sb("a_stats", [P, KT, 6])
        a_meanvar = sb("a_meanvar", [P, KT, 2])
        a_var_eps = sb("a_var_eps", [P, KT])
        a_rstd = sb("a_rstd", [P, KT])
        a_xn = sb("a_xn", [P, KT, D])
        a_xt_hi = sb("a_xt_hi", [P, L], BF16)
        a_xt_lo = sb("a_xt_lo", [P, L], BF16)
        q_op = sb("q_op", [P, 2, G, L], BF16)
        k_op = sb("k_op", [P, 2, G, L], BF16)
        q_sel = sb("q_sel", [P, 2, 2 * L], BF16)
        k_sel = sb("k_sel", [P, 2, 2 * L], BF16)
        v_op = sb("v_op", [P, 2, KT, H, 32])
        dump = sb("dump", [P, 4, L], BF16)
        row_max = sb("row_max", [P, 2, 2, KT, J])
        max_cols = sb("max_cols", [P, 2, 2, KT, J, 32], BF16)
        probs = sb("probs", [P, 2, J, 2 * L])
        ot_sb = sb("ot_sb", [P, G, L])
        rden = sb("rden", [P, KT, H])
        o_n = sb("o_n", [P, KT, D])
        o_hi = sb("o_hi", [P, L], BF16)
        o_lo = sb("o_lo", [P, L], BF16)
        o_b = sb("o_b", [P, KT, D])

        banks = ctx.enter_context(nc.psum_tensor("banks", [P, 8, 512], F32))

        x0_in, x1_in, x2_in = sem("x0_in"), sem("x1_in"), sem("x2_in")
        consts_in, w1_in, w2_in, gate_in, attn_in = (
            sem("consts_in"), sem("w1_in"), sem("w2_in"), sem("gate_in"), sem("attn_in"))
        bias_moved, out_stored = sem("bias_moved"), sem("out_stored")
        pool_set, dve_set, ffn_ready, attn_ready, bias_ready = (
            sem("pool_set"), sem("dve_set"), sem("ffn_ready"), sem("attn_ready"), sem("bias_ready"))
        attn_done = sem("attn_done")
        waits_met = sem("waits_met")

        def ffn_sems(k):
            names = ("stats_done var_ready rstd_ready rstd_step xn_ready xn_turned xtf_ready xt_step "
                     "xt_ready up_done h_ready lo_dve lo_pool down_done y_added gate_done "
                     "logits_read route_step gap_ready tanh_ready weight_step zero_added").split()
            return {n: sem(f"f{k}_{n}") for n in names}

        F = [ffn_sems(1), ffn_sems(2)]
        A = {n: sem(f"a_{n}") for n in (
            "stats_done var_ready rstd_ready rstd_step xn_ready xn_turned xt_hi_ready xt_ready "
            "k_done k_sel_ready k_ready q_done q_sel_ready q_ready v_done v_ready "
            "raw_done max_done max_step cols_ready cols_turned shift_ready "
            "st_done exp_done pv_done ot_ready ot_turned rden_step o_ready "
            "on_turned o_hi_ready o_ready2 proj_done biased x_added").split()}

        def tile_cols(t, n=1):
            return x_all[:, bass.ds(t * D, n * D)]

        block = ctx.enter_context(nc.Block())

        @block.sync
        def _(sp):
            x_tiles = x.rearrange("(n p) d -> p n d", p=P)
            xv = x_all[:].rearrange("p (n d) -> p n d", d=D)
            sp.dma_start(xv[:, 0:BT, :], x_tiles[:, 0:BT, :]).then_inc(x0_in, 16)
            sp.dma_start(ident_f[:], ident).then_inc(consts_in, 16)
            sp.dma_start(gate_t[:], gate).then_inc(gate_in, 16)
            sp.dma_start(ebias_b[:], ebias.broadcast_to([P, E])).then_inc(gate_in, 16)
            sp.dma_start(w1_f[:], w1).then_inc(w1_in, 16)
            sp.dma_start(w2_f[:], w2).then_inc(w2_in, 16)
            sp.dma_start(xv[:, BT:4 * BT, :], x_tiles[:, BT:4 * BT, :]).then_inc(x1_in, 16)
            for n, w in enumerate((wq, wk, wv, wo)):
                sp.dma_start(wstage[:, n, :], w).then_inc(attn_in, 16)
            sp.dma_start(bstage[:, 0, :], bq).then_inc(attn_in, 16)
            sp.dma_start(bstage[:, 1, :], bk).then_inc(attn_in, 16)
            sp.dma_start(bv_b[:], bv.broadcast_to([P, D])).then_inc(attn_in, 16)
            sp.dma_start(bo_b[:], bo.broadcast_to([P, D])).then_inc(attn_in, 16)
            sp.dma_start(lam_b[:], lam.broadcast_to([P, 1])).then_inc(attn_in, 16)
            sp.dma_start(prior_f[:], prior.rearrange("(t p) c -> p t c", p=P)).then_inc(attn_in, 16)
            sp.dma_start(xv[:, 4 * BT:TILES, :], x_tiles[:, 4 * BT:TILES, :]).then_inc(x2_in, 16)
            sp.wait_ge(bias_ready, 1)
            for r in range(3):
                sp.dma_start(bias_rows[r:r + 1], bias_p[:, r]).then_inc(bias_moved, 16)
            out_tiles = out.rearrange("(n p) d -> p n d", p=P)
            with sp.Fori(0, NB) as b:
                sp.wait_ge(F[1]["y_added"], FE * (b + 1))
                sp.dma_start(out_tiles[:, bass.ds(b * BT, BT), :],
                             xv[:, bass.ds(b * BT, BT), :]).then_inc(out_stored, 16)
            sp.wait_ge(out_stored, 16 * NB)

        @block.tensor
        def _(pe):
            U, Y, TX, GL = (0, 1, 2, 3), (4, 5), 6, 7

            def ffn_look_ahead(S, b):
                wait(pe, S["xn_ready"], b + 1)
                wait(pe, S["xtf_ready"], b)
                for t in range(BT):
                    mm = pe.transpose(banks[:, TX, bass.ts(t, P)], xn[:, t, :], ident_f[:])
                mm.then_inc(S["xn_turned"], 1)

            def ffn_logits(S, b):
                wait(pe, S["xtf_ready"], b + 1)
                wait(pe, S["logits_read"], b)
                for t in range(BT):
                    mm = pe.matmul(banks[:, GL, bass.ts(t, E)], xt_f[:, bass.ts(t, P)], gate_t[:],
                                   start=True, stop=True)
                mm.then_inc(S["gate_done"], 1)

            def ffn_up(S, b, e):
                for half in range(2):
                    c = 2 * e + half
                    wait(pe, S["h_ready"], 2 * FE * b + c - 3)
                    o = banks[:, U[c % 4], :]
                    pe.matmul(o, w1_hi[:, c, :], xt_hi[:], start=True, stop=False)
                    pe.matmul(o, w1_hi[:, c, :], xt_lo[:], start=False, stop=False)
                    pe.matmul(o, w1_lo[:, c, :], xt_hi[:], start=False, stop=True).then_inc(S["up_done"], 1)

            def ffn_down(S, b, e):
                m = FE * b + e
                wait(pe, S["h_ready"], 2 * m + 2)
                wait(pe, S["lo_pool"], m + 1)
                wait(pe, S["lo_dve"], m + 1)
                wait(pe, S["y_added"], m - 1)
                for t in range(BT):
                    o = banks[:, Y[e % 2], bass.ts(t, P)]
                    for half in range(2):
                        c = 2 * e + half
                        hi, lo = h_hi[:, e % 2, half, bass.ts(t, P)], h_lo[:, e % 2, half, bass.ts(t, P)]
                        pe.matmul(o, hi, w2_hi[:, c, :], start=half == 0, stop=False)
                        pe.matmul(o, hi, w2_lo[:, c, :], start=False, stop=False)
                        mm = pe.matmul(o, lo, w2_hi[:, c, :], start=False, stop=half == 1)
                mm.then_inc(S["down_done"], 1)

            def ffn_turn(S, b, before=True):
                wait(pe, S["xt_ready"], b + 1)
                for e in range(FE):
                    ffn_up(S, b, e)
                    if e == 4:
                        ffn_look_ahead(S, b + 1)
                    if e > 0:
                        ffn_down(S, b, e - 1)
                    elif before:
                        ffn_down(S, b - 1, FE - 1)
                    if e == 6:
                        ffn_logits(S, b + 1)

            def ffn(S):
                ffn_look_ahead(S, 0)
                ffn_logits(S, 0)
                ffn_turn(S, 0, before=False)
                with pe.Fori(1, NB) as b:
                    ffn_turn(S, b)
                ffn_down(S, NB - 1, FE - 1)

            pe.wait_ge(consts_in, 16)
            pe.wait_ge(gate_in, 32)
            pe.wait_ge(ffn_ready, 1)
            ffn(F[0])

            ST, MX, PV, M = (0, 1), (2, 3), (4, 5), (6, 7)
            pe.wait_ge(attn_ready, 1)
            pe.wait_ge(bias_moved, 48)
            pe.wait_ge(F[0]["y_added"], FE * NB)

            def project(o, w_hi, w_lo, which, g2, done):
                for k in range(2):
                    g = 2 * g2 + k
                    cols = o[:, bass.ts(k, L)]
                    wh = w_hi[:, J * g:J * g + J, :].rearrange("p j c -> p (j c)")
                    wl = w_lo[:, J * g:J * g + J, :].rearrange("p j c -> p (j c)")
                    br = bias_rows[:, which, J * g:J * g + J, :].rearrange("p j c -> p (j c)")
                    pe.matmul(cols, wh, a_xt_hi[:], start=True, stop=False)
                    pe.matmul(cols, wh, a_xt_lo[:], start=False, stop=False)
                    pe.matmul(cols, wl, a_xt_hi[:], start=False, stop=False)
                    mm = pe.matmul(cols, br, ones_row[:], start=False, stop=True)
                mm.then_inc(done, 1)

            def raw_scores(b, par, v):
                gp, qt, j = v // 8, v % 8 // 4, v % 4
                wait(pe, A["q_ready"], 2 * b + gp + 1)
                wait(pe, A["k_ready"], 2 * b + gp + 1)
                wait(pe, A["max_done"], 16 * b + v - 1)
                for k in range(2):
                    r, g = 32 * j, 2 * gp + k
                    mm = pe.matmul(banks[:, MX[v % 2], bass.ts(k, L)],
                                   q_op[r:r + 32, par, g, bass.ts(qt, P)], k_op[r:r + 32, par, g, :],
                                   start=True, stop=True)
                mm.then_inc(A["raw_done"], 1)

            def scores(b, par, u):
                gp, kt, j = u // 8, u % 8 // 4, u % 4
                wait(pe, A["shift_ready"], 2 * b + gp + 1)
                wait(pe, A["exp_done"], 16 * b + u - 1)
                o = banks[:, ST[u % 2], :]
                for k in range(2):
                    r, g = 32 * j, 2 * gp + k
                    o = banks[:, ST[u % 2], bass.ts(k, L)]
                    pe.matmul(o, ident_r[:], prior_hi[:, kt, :], start=True, stop=False)
                    pe.matmul(o, ident_r[:], prior_lo[:, kt, :], start=False, stop=False)
                    mm = pe.matmul(o,
                                   k_op[r:r + 32, par, g, bass.ts(kt, P)], q_op[r:r + 32, par, g, :],
                                   start=False, stop=True)
                mm.then_inc(A["st_done"], 1)

            def weighted(b, par, w):
                gp, kt, k = w // 4, w % 4 // 2, w % 2
                wait(pe, A["exp_done"], 16 * b + 4 * (w // 2) + 4)
                if w == 0:
                    wait(pe, A["v_ready"], b + 1)
                    wait(pe, A["ot_ready"], 2 * b - 1)
                if w == 4:
                    wait(pe, A["ot_ready"], 2 * b)
                for j in range(J):
                    mm = pe.matmul(banks[32 * j:32 * j + 32, PV[gp], bass.ts(k, L)],
                                   v_op[:, par, kt, J * (2 * gp + k) + j, :],
                                   probs[:, w // 2 % 2, j, bass.ts(k, L)],
                                   start=kt == 0 and k == 0, stop=kt == 1, skip_group_check=True)
                mm.then_inc(A["pv_done"], 1)

            def turn_cols(b, par, gp):
                wait(pe, A["cols_ready"], 2 * b + gp + 1)
                o = banks[:, M[gp], :].bitcast(BF16)
                for k in range(2):
                    for qt in range(KT):
                        mm = pe.transpose(o[:, bass.ts(2 * k + qt, P)],
                                          max_cols[:, gp, k, qt].rearrange("p j c -> p (j c)"), ident_h[:])
                mm.then_inc(A["cols_turned"], 1)

            def turn(b, par, ahead=True, main=True, behind=True):
                nxt = 1 - par
                for u in range(16):
                    if main:
                        scores(b, par, u)
                    if u < 4 and main:
                        raw_scores(b, par, 12 + u)
                    if u >= 4 and ahead:
                        raw_scores(b + 1, nxt, u - 4)
                    if u in (5, 6, 9, 10, 13, 14) and main:
                        weighted(b, par, 2 * ((u - 5) // 4) + (u - 5) % 4)
                    if u in (1, 2) and behind:
                        weighted(b - 1, nxt, 5 + u)
                    if u == 0 and ahead:
                        wait(pe, A["xn_ready"], b + 2)
                        wait(pe, A["shift_ready"], 2 * b + 1)
                        for t in range(KT):
                            mm = pe.transpose(banks[:, M[0], bass.ts(t, P)], a_xn[:, t, :], ident_f[:])
                        mm.then_inc(A["xn_turned"], 1)
                    if u == 1 and ahead:
                        wait(pe, A["xt_ready"], b + 2)
                        project(banks[:, M[0], :], wk_hi, wk_lo, 1, 0, A["k_done"])
                    if u == 2 and ahead:
                        wait(pe, A["q_ready"], 2 * b + 2)
                        wait(pe, A["o_ready2"], b - 1)
                        project(banks[:, M[1], :], wk_hi, wk_lo, 1, 1, A["k_done"])
                        wait(pe, A["k_ready"], 2 * b + 3)
                        project(banks[:, M[0], :], wq_hi, wq_lo, 0, 0, A["q_done"])
                    if u == 3 and ahead:
                        wait(pe, A["k_ready"], 2 * b + 4)
                        project(banks[:, M[1], :], wq_hi, wq_lo, 0, 1, A["q_done"])
                    if u == 4 and ahead:
                        wait(pe, A["q_ready"], 2 * b + 3)
                        for t in range(KT):
                            o = banks[:, M[0], bass.ts(t, P)]
                            pe.matmul(o, a_xt_hi[:, bass.ts(t, P)], wv_hi[:], start=True, stop=False)
                            pe.matmul(o, a_xt_hi[:, bass.ts(t, P)], wv_lo[:], start=False, stop=False)
                            mm = pe.matmul(o, a_xt_lo[:, bass.ts(t, P)], wv_hi[:], start=False, stop=True)
                        mm.then_inc(A["v_done"], 1)
                    if u == 5 and main:
                        if ahead:
                            wait(pe, A["q_ready"], 2 * b + 4)
                        wait(pe, A["o_ready2"], b - 1)
                        turn_cols(b, par, 1)
                    if u in (6, 7) and behind:
                        qt = u - 6
                        wait(pe, A["ot_ready"], 2 * b)
                        if qt == 0:
                            wait(pe, A["v_ready"], b + 2 if ahead else NBATCH)
                            wait(pe, A["biased"], b - 1)
                        if qt == 1:
                            wait(pe, A["shift_ready"], 2 * b + 2 if main else 2 * b)
                            wait(pe, A["o_ready2"], b - 1)
                        for g in range(G):
                            mm = pe.transpose(banks[:, M[qt], bass.ts(g, P)],
                                              ot_sb[:, g, bass.ts(qt, P)], ident_f[:])
                        mm.then_inc(A["ot_turned"], 1)
                    if u == 9 and behind:
                        wait(pe, A["o_ready"], 2 * b)
                        for t in range(KT):
                            mm = pe.transpose(banks[:, M[1], bass.ts(t, P)], o_n[:, t, :], ident_f[:])
                        mm.then_inc(A["on_turned"], 1)
                    if u == 11 and behind:
                        wait(pe, A["o_ready2"], b)
                        for t in range(KT):
                            o = banks[:, M[0], bass.ts(t, P)]
                            pe.matmul(o, o_hi[:, bass.ts(t, P)], wo_hi[:], start=True, stop=False)
                            pe.matmul(o, o_hi[:, bass.ts(t, P)], wo_lo[:], start=False, stop=False)
                            mm = pe.matmul(o, o_lo[:, bass.ts(t, P)], wo_hi[:], start=False, stop=True)
                        mm.then_inc(A["proj_done"], 1)
                    if u == 13 and ahead:
                        if behind:
                            wait(pe, A["biased"], b)
                        wait(pe, A["v_ready"], b + 2)
                        turn_cols(b + 1, nxt, 0)

            turn(-1, 1, main=False, behind=False)
            turn(0, 0, behind=False)
            turn(1, 1)
            turn(2, 0)
            with pe.Fori(1, NBATCH // 2 - 1) as i:
                turn(2 * i + 1, 1)
                turn(2 * i + 2, 0)
            turn(NBATCH - 1, 1, ahead=False)
            turn(NBATCH, 0, ahead=False, main=False)

            pe.wait_ge(attn_done, 1)
            ffn(F[1])

        @block.scalar
        def _(act):
            U, TX = (0, 1, 2, 3), 6

            def ffn_xt(S, b):
                wait(act, S["xn_turned"], b + 1)
                wait(act, S["gate_done"], b)
                wait(act, S["xt_ready"], b)
                act.activation(xt_f[:], banks[:, TX, :], ACT.Copy).then_inc(S["xtf_ready"], 1)

            def ffn_tanh(S, b):
                wait(act, S["gap_ready"], b + 1)
                wait(act, S["weight_step"], 5 * b)
                act.activation(tanh_gap[:], gap[:], ACT.Tanh, scale=0.5).then_inc(S["tanh_ready"], 1)

            def ffn_turn(S, b):
                for e in range(FE):
                    m = FE * b + e
                    for half in range(2):
                        c = 2 * e + half
                        wait(act, S["up_done"], 2 * FE * b + c + 1)
                        wait(act, S["lo_pool" if half == 0 else "lo_dve"], m - 1)
                        act.activation(h_f[:, e % 2, half, :], banks[:, U[c % 4], :], ACT.Silu)
                        wait(act, S["down_done"], m - 1)
                        act.activation(h_hi[:, e % 2, half, :], banks[:, U[c % 4], :],
                                       ACT.Silu).then_inc(S["h_ready"], 1)
                    if e == 5:
                        ffn_xt(S, b + 1)
                ffn_tanh(S, b + 1)

            def ffn(S):
                ffn_xt(S, 0)
                ffn_tanh(S, 0)
                ffn_turn(S, 0)
                with act.Fori(1, NB) as b:
                    ffn_turn(S, b)

            ffn(F[0])

            ST, PV, M = (0, 1), (4, 5), (6, 7)
            act.wait_ge(attn_ready, 1)
            act.wait_ge(F[0]["y_added"], FE * NB)

            def turn(b, par, ahead=True, main=True, behind=True):
                nxt = 1 - par
                for u in range(16):
                    if main:
                        q = u // 4
                        wait(act, A["st_done"], 16 * b + u + 1)
                        wait(act, A["pv_done"], 8 * b + 2 * q - 2)
                        act.activation(probs[:, q % 2, u % 4, :], banks[:, ST[u % 2], :],
                                       ACT.Exp).then_inc(A["exp_done"], 1)
                    if u == 0 and ahead:
                        wait(act, A["xn_turned"], b + 2)
                        wait(act, A["v_done"], b + 1)
                        act.activation(a_xt_hi[:], banks[:, M[0], 0:L], ACT.Copy).then_inc(A["xt_hi_ready"], 1)
                    if u in (1, 2) and ahead:
                        n = 2 * (b + 1) + u - 1
                        wait(act, A["k_done"], n + 1)
                        wait(act, A["k_ready"], n - 1)
                        act.activation(k_sel[:, u - 1, :], banks[:, M[u - 1], :], ACT.Copy,
                                       scale=neg_lo[:, 1:2]).then_inc(A["k_sel_ready"], 1)
                    if u in (2, 3) and ahead:
                        n = 2 * (b + 1) + u - 2
                        wait(act, A["q_done"], n + 1)
                        wait(act, A["q_ready"], n - 1)
                        act.activation(q_sel[:, u - 2, :], banks[:, M[u - 2], :], ACT.Copy,
                                       scale=neg_lo[:, 0:1]).then_inc(A["q_sel_ready"], 1)
                    if u == 3 and behind:
                        wait(act, A["pv_done"], 8 * b)
                        wait(act, A["ot_turned"], 2 * b - 2)
                        act.activation(ot_sb[:, 2:4, :].rearrange("p g c -> p (g c)"),
                                       banks[:, PV[1], :], ACT.Copy).then_inc(A["ot_ready"], 1)
                    if u == 10 and behind:
                        wait(act, A["on_turned"], b)
                        wait(act, A["proj_done"], b - 1)
                        act.activation(o_hi[:], banks[:, M[1], 0:L], ACT.Copy).then_inc(A["o_hi_ready"], 1)
                    if u == 11 and main:
                        wait(act, A["pv_done"], 8 * b + 4)
                        wait(act, A["ot_turned"], 2 * b)
                        act.activation(ot_sb[:, 0:2, :].rearrange("p g c -> p (g c)"),
                                       banks[:, PV[0], :], ACT.Copy).then_inc(A["ot_ready"], 1)

            turn(-1, 1, main=False, behind=False)
            turn(0, 0, behind=False)
            turn(1, 1)
            turn(2, 0)
            with act.Fori(1, NBATCH // 2 - 1) as i:
                turn(2 * i + 1, 1)
                turn(2 * i + 2, 0)
            turn(NBATCH - 1, 1, ahead=False)
            turn(NBATCH, 0, ahead=False, main=False)

            act.wait_ge(attn_done, 1)
            ffn(F[1])

        @block.gpsimd
        def _(pool):
            pool.memset(x_all[:, TILES * D:], 0.0)
            pool.memset(neg_half[:], -0.5)
            pool.memset(wq_hi[:], 0.0)
            pool.memset(wq_lo[:], 0.0)
            pool.memset(wk_hi[:], 0.0)
            pool.memset(wk_lo[:], 0.0)
            pool.memset(bias_f[:], 0.0)
            pool.memset(ones_row[:], 1.0)
            pool.memset(max_cols[:], 0.0)
            pool.memset(v_op[:], 0.0)
            pool.iota(rank[:], pattern=[[-1, E]], base=E, channel_multiplier=0,
                      allow_small_or_imprecise_dtypes=True).then_inc(pool_set, 1)
            pool.wait_ge(pool_set, 1)
            pool.memset(v_op[:, :, :, :, HD:HD + 1], 1.0)
            pool.memset(bias_f[:, 1, :, 3 * HD:3 * HD + 2], 1.0).then_inc(pool_set, 1)

            def root(S, b, n, ve, rs, mv, tag):
                wait(pool, S["var_ready"], b + 1)
                alone(pool, waits_met)
                pool.tensor_scalar(ve[:], mv[:, :, 1], EPS, 1.0, ALU.add, ALU.mult).then_inc(S["rstd_step"], 1)
                wait(pool, S["rstd_step"], b + 1)
                wait(pool, S["xn_ready"], b)
                pool.tensor_tensor(rs[:], ve[:], neg_half[:, 0:n], ALU.pow).then_inc(S["rstd_ready"], 1)

            def ffn_turn(S, b):
                for e in range(FE):
                    m = FE * b + e
                    wait(pool, S["h_ready"], 2 * m + 1)
                    wait(pool, S["down_done"], m - 1)
                    pool.tensor_tensor(h_lo[:, e % 2, 0, :], h_f[:, e % 2, 0, :], h_hi[:, e % 2, 0, :],
                                       ALU.subtract).then_inc(S["lo_pool"], 1)
                    if e == 1:
                        root(S, b + 1, BT, var_eps, rstd, meanvar, "f")

            def ffn(S):
                root(S, 0, BT, var_eps, rstd, meanvar, "f")
                ffn_turn(S, 0)
                with pool.Fori(1, NB) as b:
                    ffn_turn(S, b)

            ffn(F[0])
            root(A, 0, KT, a_var_eps, a_rstd, a_meanvar, "a")
            with pool.Fori(1, NBATCH + 1) as b:
                root(A, b, KT, a_var_eps, a_rstd, a_meanvar, "a")
            pool.wait_ge(attn_done, 1)
            ffn(F[1])

        @block.vector
        def _(dve):
            Y, TX, GL = (4, 5), 6, 7

            def norm_stats(S, b, tile0, n, st, mv):
                wait(dve, S["stats_done"], b)
                for t in range(n):
                    i = dve.bn_stats(st[:, t, :], tile_cols(tile0 + t))
                i.then_inc(S["stats_done"], 1)
                wait(dve, S["stats_done"], b + 1)
                wait(dve, S["rstd_step"], b)
                alone(dve, waits_met)
                for t in range(n):
                    i = dve.bn_aggr(mv[:, t, :], st[:, t, :])
                i.then_inc(S["var_ready"], 1)

            def norm_apply(S, b, tile0, n, mv, rs, dst):
                wait(dve, S["var_ready"], b + 1)
                wait(dve, S["rstd_ready"], b + 1)
                wait(dve, S["xn_turned"], b)
                for t in range(n):
                    i = dve.tensor_scalar(dst[:, t, :], tile_cols(tile0 + t), mv[:, t, 0:1], rs[:, t:t + 1],
                                          ALU.subtract, ALU.mult)
                i.then_inc(S["xn_ready"], 1)

            def route_pick(S, b):
                step = [0]

                def link(ins):
                    step[0] += 1
                    ins.then_inc(S["route_step"], 1)
                    wait(dve, S["route_step"], 10 * b + step[0])

                wait(dve, S["gate_done"], b + 1)
                wait(dve, S["weight_step"], 5 * b)
                dve.tensor_tensor(logits[:], banks[:, GL, 0:BT * E].rearrange("p (t e) -> p t e", e=E),
                                  bc(ebias_b[:], 1, BT), ALU.add).then_inc(S["logits_read"], 1)
                wait(dve, S["logits_read"], b + 1)
                link(dve.tensor_reduce(top0[:], logits[:], AX.X, ALU.max))
                link(dve.tensor_tensor(eq[:], logits[:], bc(top0[:], 2, E), ALU.is_equal))
                link(dve.tensor_tensor(ranked[:], eq[:], bc(rank[:], 1, BT), ALU.mult))
                link(dve.tensor_reduce(first[:], ranked[:], AX.X, ALU.max))
                link(dve.tensor_tensor(hot0[:], bc(rank[:], 1, BT), bc(first[:], 2, E), ALU.is_equal))
                link(dve.scalar_tensor_tensor(masked[:], hot0[:], LOWEST, logits[:], ALU.mult, ALU.add))
                link(dve.tensor_reduce(top1[:], masked[:], AX.X, ALU.max))
                dve.tensor_tensor(gap[:], top0[:], top1[:], ALU.subtract).then_inc(S["gap_ready"], 1)
                link(dve.tensor_tensor(eq[:], masked[:], bc(top1[:], 2, E), ALU.is_equal))
                link(dve.tensor_tensor(ranked[:], eq[:], bc(rank[:], 1, BT), ALU.mult))
                link(dve.tensor_reduce(first[:], ranked[:], AX.X, ALU.max))
                assert step[0] == 10
                dve.tensor_tensor(hot1[:], bc(rank[:], 1, BT), bc(first[:], 2, E),
                                  ALU.is_equal).then_inc(S["xt_step"], 1)

            def route_weigh(S, b):
                wait(dve, S["tanh_ready"], b + 1)
                wait(dve, S["xt_step"], 2 * b + 1)
                wait(dve, S["zero_added"], b)
                dve.tensor_scalar(half_w0[:], tanh_gap[:], 0.25, 0.25, ALU.mult, ALU.add)
                dve.tensor_scalar(half_w1[:], tanh_gap[:], -0.25, 0.25, ALU.mult,
                                  ALU.add).then_inc(S["weight_step"], 1)
                wait(dve, S["weight_step"], 5 * b + 1)
                dve.tensor_tensor(part0[:], hot0[:], bc(half_w0[:], 2, E), ALU.mult).then_inc(S["weight_step"], 1)
                dve.tensor_tensor(part1[:], hot1[:], bc(half_w1[:], 2, E), ALU.mult).then_inc(S["weight_step"], 1)
                wait(dve, S["weight_step"], 5 * b + 3)
                wait(dve, S["y_added"], FE * b)
                dve.tensor_tensor(w_tok[:], part0[:], part1[:], ALU.add).then_inc(S["weight_step"], 1)
                wait(dve, S["weight_step"], 5 * b + 4)
                dve.tensor_reduce(w_zero[:], w_tok[:, :, FE:E], AX.X, ALU.add).then_inc(S["weight_step"], 1)
                wait(dve, S["weight_step"], 5 * b + 5)

            def add_expert(S, b, e):
                m = FE * b + e
                wait(dve, S["down_done"], m + 1)
                wait(dve, S["y_added"], m)
                if e == 0:
                    wait(dve, S["zero_added"], b + 1)
                for t in range(BT):
                    xt = tile_cols(BT * b + t)
                    i = dve.scalar_tensor_tensor(xt, banks[:, Y[e % 2], bass.ts(t, P)], w_tok[:, t, e:e + 1],
                                                 xt, ALU.mult, ALU.add)
                i.then_inc(S["y_added"], 1)

            def ffn_turn(S, b, before=True):
                wait(dve, S["xtf_ready"], b + 1)
                wait(dve, S["up_done"], 2 * FE * b)
                dve.tensor_copy(xt_hi[:], xt_f[:]).then_inc(S["xt_step"], 1)
                wait(dve, S["xt_step"], 2 * b + 2)
                dve.tensor_tensor(xt_lo[:], xt_f[:], xt_hi[:], ALU.subtract).then_inc(S["xt_ready"], 1)
                for e in range(FE):
                    m = FE * b + e
                    wait(dve, S["h_ready"], 2 * m + 2)
                    wait(dve, S["down_done"], m - 1)
                    dve.tensor_tensor(h_lo[:, e % 2, 1, :], h_f[:, e % 2, 1, :], h_hi[:, e % 2, 1, :],
                                      ALU.subtract).then_inc(S["lo_dve"], 1)
                    if e > 0:
                        add_expert(S, b, e - 1)
                    else:
                        if before:
                            add_expert(S, b - 1, FE - 1)
                        route_weigh(S, b)
                        for t in range(BT):
                            xt = tile_cols(BT * b + t)
                            i = dve.scalar_tensor_tensor(xt, xn[:, t, :], w_zero[:, t:t + 1], xt,
                                                         ALU.mult, ALU.add)
                        i.then_inc(S["zero_added"], 1)
                    if e == 1:
                        norm_stats(S, b + 1, BT * (b + 1), BT, stats, meanvar)
                    if e == 3:
                        wait(dve, S["zero_added"], b + 1)
                        norm_apply(S, b + 1, BT * (b + 1), BT, meanvar, rstd, xn)
                route_pick(S, b + 1)

            def ffn(S, loads=False):
                norm_stats(S, 0, 0, BT, stats, meanvar)
                norm_apply(S, 0, 0, BT, meanvar, rstd, xn)
                route_pick(S, 0)
                if loads:
                    dve.wait_ge(x1_in, 16)
                ffn_turn(S, 0, before=False)
                if loads:
                    dve.wait_ge(x2_in, 16)
                with dve.Fori(1, NB) as b:
                    ffn_turn(S, b)
                add_expert(S, NB - 1, FE - 1)

            def split(hi, lo, src):
                n[0] += 1
                dve.tensor_copy(hi, src).then_inc(dve_set, 1)
                dve.wait_ge(dve_set, n[0])
                return dve.tensor_tensor(lo, src, hi, ALU.subtract)

            n = [0]
            dve.wait_ge(x0_in, 16)
            dve.wait_ge(pool_set, 2)
            dve.wait_ge(consts_in, 16)
            dve.wait_ge(w1_in, 16)
            split(w1_hi[:].rearrange("p c f -> p (c f)"), w1_lo[:].rearrange("p c f -> p (c f)"), w1_f[:])
            dve.wait_ge(w2_in, 16)
            dve.wait_ge(gate_in, 32)
            split(w2_hi[:].rearrange("p c f -> p (c f)"), w2_lo[:].rearrange("p c f -> p (c f)"),
                  w2_f[:]).then_inc(ffn_ready, 1)
            dve.wait_ge(attn_in, 160)
            n[0] += 1
            dve.tensor_scalar(wq_s[:], wstage[:, 0, :], QSCALE, None, ALU.mult).then_inc(dve_set, 1)
            dve.wait_ge(dve_set, n[0])
            for src, hi, lo in ((wq_s[:], wq_hi, wq_lo), (wstage[:, 1, :], wk_hi, wk_lo)):
                s3 = src.rearrange("p (h d) -> p h d", d=HD)
                for r in range(3):
                    split(hi[:, :, HD * r:HD * r + HD], lo[:, :, HD * r:HD * r + HD], s3)
            split(wv_hi[:], wv_lo[:], wstage[:, 2, :])
            split(wo_hi[:], wo_lo[:], wstage[:, 3, :])
            for r in range(3):
                dve.tensor_scalar(bias_f[:, 0, :, HD * r:HD * r + HD],
                                  bstage[:, 0, :].rearrange("p (h d) -> p h d", d=HD), QSCALE, None, ALU.mult)
                i = dve.tensor_copy(bias_f[:, 1, :, HD * r:HD * r + HD],
                                    bstage[:, 1, :].rearrange("p (h d) -> p h d", d=HD))
            n[0] += 1
            i.then_inc(dve_set, 1)
            dve.wait_ge(dve_set, n[0])
            for r, (src, rest) in enumerate(((bias_f, bias_r), (bias_r, bias_f), (bias_f, None))):
                n[0] += 1
                i = dve.tensor_copy(bias_p[:, r], src[:])
                i.then_inc(dve_set, 1)
                dve.wait_ge(dve_set, n[0])
                if rest is not None:
                    n[0] += 1
                    dve.tensor_tensor(rest[:], src[:], bias_p[:, r], ALU.subtract).then_inc(dve_set, 1)
                    dve.wait_ge(dve_set, n[0])
                else:
                    dve.tensor_copy(ident_h[:], ident_f[:]).then_inc(bias_ready, 1)
            dve.tensor_copy(ident_r[:], ident_f[:])
            iv = ident_f[:].rearrange("p (j c) -> p j c", c=32)
            dve.tensor_reduce(neg_lo[:, 0:1], iv[:, :, HD:2 * HD], AX.XY, ALU.add, negate=True)
            dve.tensor_reduce(neg_lo[:, 1:2], iv[:, :, 2 * HD:3 * HD], AX.XY, ALU.add, negate=True)
            n[0] += 1
            dve.tensor_scalar(prior_f[:], prior_f[:], lam_b[:, 0:1], None, ALU.mult).then_inc(dve_set, 1)
            dve.wait_ge(dve_set, n[0])
            n[0] += 1
            dve.tensor_copy(prior_hi[:], prior_f[:]).then_inc(dve_set, 1)
            dve.wait_ge(dve_set, n[0])
            dve.tensor_tensor(prior_lo[:], prior_f[:], prior_hi[:].bitcast(F32), ALU.subtract).then_inc(attn_ready, 1)

            ffn(F[0], loads=True)

            MX, M = (2, 3), (6, 7)

            def batch_stats(b):
                norm_stats(A, b, KT * b, KT, a_stats, a_meanvar)

            def batch_norm(b):
                norm_apply(A, b, KT * b, KT, a_meanvar, a_rstd, a_xn)

            def maxima(b, v):
                gp, qt, j = v // 8, v % 8 // 4, v % 4
                wait(dve, A["raw_done"], 16 * b + v + 1)
                wait(dve, A["max_done"], 16 * b + v - 1)
                if v % 8 == 0:
                    wait(dve, A["cols_ready"], 2 * b + gp - 1)
                alone(dve, waits_met)
                for k in range(2):
                    i = dve.tensor_tensor_reduce(dump[:, 2 * (v % 2) + k, :], banks[:, MX[v % 2], bass.ts(k, L)],
                                                 prior_f[:, qt, :], 1.0, LOWEST, ALU.add, ALU.max,
                                                 row_max[:, gp, k, qt, j:j + 1])
                i.then_inc(A["max_done"], 1)

            def columns(b, gp):
                wait(dve, A["max_done"], 16 * b + 8 * gp + 8)
                wait(dve, A["cols_turned"], 2 * b + gp - 1)
                rm = row_max[:, gp].rearrange("p k t j -> p (k t) j")
                mc = max_cols[:, gp].rearrange("p k t j c -> p (k t) j c")
                hi, lo = mc[:, :, :, 3 * HD], mc[:, :, :, 3 * HD + 1]
                dve.tensor_scalar(hi, rm, -1.0, None, ALU.mult).then_inc(A["max_step"], 1)
                wait(dve, A["max_step"], 2 * b + gp + 1)
                dve.scalar_tensor_tensor(lo, rm, -1.0, hi, ALU.mult, ALU.subtract).then_inc(A["cols_ready"], 1)

            def merge(b, par, gp):
                wait(dve, A["cols_turned"], 2 * b + gp + 1)
                wait(dve, A["max_done"], 16 * b + 8 * gp + 8)
                q = q_op[:, par, 2 * gp:2 * gp + 2, :].rearrange("p g c -> p (g c)")
                dve.tensor_tensor(q, banks[:, M[gp], :].bitcast(BF16)[:, 0:2 * L], q,
                                  ALU.add).then_inc(A["shift_ready"], 1)

            def operand(kind, dst, sel, b, nxt, g2):
                wait(dve, A[kind + "_sel_ready"], 2 * (b + 1) + g2 + 1)
                dve.tensor_tensor(dst[:, nxt, 2 * g2:2 * g2 + 2, :].rearrange("p g c -> p (g c)"),
                                  banks[:, M[g2], :], sel[:, g2, :], ALU.add).then_inc(A[kind + "_ready"], 1)

            def turn(b, par, ahead=True, main=True, behind=True):
                nxt = 1 - par
                for u in range(16):
                    if u < 4 and main:
                        maxima(b, 12 + u)
                    if u >= 4 and ahead:
                        maxima(b + 1, u - 4)
                    if u == 3 and main:
                        columns(b, 1)
                    if u == 11 and ahead:
                        columns(b + 1, 0)
                    if u == 0 and ahead:
                        wait(dve, A["xt_hi_ready"], b + 2)
                        dve.tensor_tensor(a_xt_lo[:], banks[:, M[0], 0:L], a_xt_hi[:],
                                          ALU.subtract).then_inc(A["xt_ready"], 1)
                    if u in (1, 2) and ahead:
                        operand("k", k_op, k_sel, b, nxt, u - 1)
                    if u in (2, 3) and ahead:
                        operand("q", q_op, q_sel, b, nxt, u - 2)
                    if u == 4 and ahead:
                        wait(dve, A["v_done"], b + 2)
                        for t in range(KT):
                            i = dve.tensor_tensor(v_op[:, nxt, t, :, 0:HD],
                                                  banks[:, M[0], bass.ts(t, P)].rearrange("p (h d) -> p h d", d=HD),
                                                  bv_b[:].rearrange("p (h d) -> p h d", d=HD), ALU.add)
                        i.then_inc(A["v_ready"], 1)
                    if u == 5 and main:
                        merge(b, par, 1)
                    if u in (6, 7) and behind:
                        qt = u - 6
                        wait(dve, A["ot_turned"], 2 * (b - 1) + qt + 1)
                        wait(dve, A["on_turned"], b - 1)
                        ov = banks[:, M[qt], :].rearrange("p (h c) -> p h c", c=32)
                        dve.reciprocal(rden[:, qt, :], ov[:, :, HD]).then_inc(A["rden_step"], 1)
                        wait(dve, A["rden_step"], 2 * (b - 1) + qt + 1)
                        dve.tensor_tensor(o_n[:, qt, :].rearrange("p (h d) -> p h d", d=HD), ov[:, :, 0:HD],
                                          bc(rden[:, qt, :], 2, HD), ALU.mult).then_inc(A["o_ready"], 1)
                    if u == 10 and behind:
                        wait(dve, A["o_hi_ready"], b)
                        wait(dve, A["proj_done"], b - 1)
                        dve.tensor_tensor(o_lo[:], banks[:, M[1], 0:L], o_hi[:],
                                          ALU.subtract).then_inc(A["o_ready2"], 1)
                    if u == 12 and behind:
                        wait(dve, A["proj_done"], b)
                        wait(dve, A["x_added"], b - 1)
                        for t in range(KT):
                            i = dve.tensor_tensor(o_b[:, t, :], banks[:, M[0], bass.ts(t, P)], bo_b[:], ALU.add)
                        i.then_inc(A["biased"], 1)
                        wait(dve, A["biased"], b)
                        xt = tile_cols(KT * (b - 1), KT)
                        dve.tensor_tensor(xt, xt, o_b[:].rearrange("p t d -> p (t d)"),
                                          ALU.add).then_inc(A["x_added"], 1)
                    if u == 12 and ahead:
                        batch_stats(b + 2) if not (isinstance(b, int) and b + 2 > NBATCH) else None
                    if u == 13 and ahead:
                        merge(b + 1, nxt, 0)
                    if u == 14 and ahead:
                        batch_norm(b + 2) if not (isinstance(b, int) and b + 2 > NBATCH) else None

            dve.wait_ge(F[0]["y_added"], FE * NB)
            batch_stats(0)
            batch_norm(0)
            turn(-1, 1, main=False, behind=False)
            turn(0, 0, behind=False)
            turn(1, 1)
            turn(2, 0)
            with dve.Fori(1, NBATCH // 2 - 1) as i:
                turn(2 * i + 1, 1)
                turn(2 * i + 2, 0)
            turn(NBATCH - 1, 1, ahead=False)
            turn(NBATCH, 0, ahead=False, main=False)
            dve.wait_ge(A["x_added"], NBATCH)
            dve.wait_ge(A["biased"], NBATCH)
            dve.memset(first[:], 0.0).then_inc(attn_done, 1)

            ffn(F[1])


def kernel(**inputs):
    import numpy as np
    import concourse.bacc as bacc
    from concourse.bass_utils import run_bass_kernel_spmd

    def f32(name):
        return np.asarray(inputs[name])

    x = f32("L0_attn_x")
    B, L, D = x.shape
    w1, w2 = f32("L0_ffn_w1"), f32("L0_ffn_w2")
    FE, F, _ = w1.shape
    pos = np.arange(L, dtype=np.float32)
    dist = np.abs(pos[:, None] - pos[None, :])
    prior = np.zeros_like(dist)
    for period, weight, sigma in ((1.0, 0.8, 0.5), (30.0, 0.4, 2.0)):
        prior = prior + np.float32(weight) * np.exp(-(dist - np.float32(period)) ** 2 / np.float32(2.0 * sigma ** 2))
    arrays = {
        "x": x.reshape(B * L, D),
        "wq": f32("L0_attn_Wq").T, "bq": f32("L0_attn_bq").reshape(1, D),
        "wk": f32("L0_attn_Wk").T, "bk": f32("L0_attn_bk").reshape(1, D),
        "wv": f32("L0_attn_Wv").T, "bv": f32("L0_attn_bv").reshape(1, D),
        "wo": f32("L0_attn_Wo").T, "bo": f32("L0_attn_bo").reshape(1, D),
        "lam": f32("L0_attn_prior_lambda").reshape(1, 1),
        "gate": f32("L0_ffn_gate_w").T,
        "ebias": f32("L0_ffn_expert_bias").reshape(1, -1),
        "w1": w1.transpose(2, 0, 1).reshape(D, FE * F),
        "w2": w2.transpose(0, 2, 1).reshape(FE * F // 128, 128, D).transpose(1, 0, 2).reshape(128, -1),
        "ident": np.eye(128, dtype=np.float32),
        "prior": prior.astype(np.float32),
    }
    arrays = {k: np.ascontiguousarray(v) for k, v in arrays.items()}
    nc = bacc.Bacc("TRN2", target_bir_lowering=False, num_devices=1)
    args = [nc.dram_tensor(f"in_{k}", v.shape, mybir.dt.from_np(v.dtype), kind="ExternalInput").ap()
            for k, v in arrays.items()]
    out = nc.dram_tensor("out", (B * L, D), F32, kind="ExternalOutput").ap()
    build(nc, *args, out)
    r = run_bass_kernel_spmd(nc, [{f"in_{k}": v for k, v in arrays.items()}], core_ids=[0])
    return r.results[0]["out"].reshape(B, L, D)
```

```python
from contextlib import ExitStack

import concourse.bass as bass
from concourse import mybir

F32 = mybir.dt.float32
F32R = mybir.dt.float32r
BF16 = mybir.dt.bfloat16
ALU = mybir.AluOpType
ACT = mybir.ActivationFunctionType
AX = mybir.AxisListType

P = 128


def wait(eng, sem, value):
    if not (isinstance(value, int) and value <= 0):
        eng.wait_ge(sem, value)


def alone(eng, waits_met):
    eng.sem_inc(waits_met, 1)


def bc(ap, axis, n):
    ap = ap.unsqueeze(axis)
    shape = list(ap.shape)
    shape[axis] = n
    return ap.broadcast_to(shape)


def build(nc, x, wq, bq, wk, bk, wv, bv, wo, bo, lam, gate, ebias, w1, w2, ident, prior, out, reach):
    N, D = x.shape
    E = gate.shape[1]
    FE = w1.shape[1] // 256
    L = prior.shape[0]
    H, HD = 16, 8
    TILES = N // P
    BT = 4
    BLK = BT * P
    NB = TILES // BT
    NBATCH = N // L
    SPARE = BT
    G, J = 4, 4
    KT = L // P
    QSCALE = float(HD) ** -0.5
    EPS = 1e-5
    LOWEST = -3.0e38
    HS = 4
    LAG = 2
    assert D == P and FE * 256 == w1.shape[1] and KT == 2 and G * J == H and E == 12

    with ExitStack() as ctx:
        def sb(name, shape, dt=F32):
            return ctx.enter_context(nc.sbuf_tensor(name, shape, dt))

        def sem(name):
            return ctx.enter_context(nc.semaphore(name))

        x_all = sb("x_all", [P, (TILES + SPARE) * D])
        w1_f = sb("w1_f", [P, FE * 256])
        w2_f = sb("w2_f", [P, FE * 2 * D])
        w1_hi = sb("w1_hi", [P, FE * 2, P], BF16)
        w1_lo = sb("w1_lo", [P, FE * 2, P], BF16)
        w2_hi = sb("w2_hi", [P, FE * 2, D], BF16)
        w2_lo = sb("w2_lo", [P, FE * 2, D], BF16)
        gate_t = sb("gate_t", [P, E])
        ebias_b = sb("ebias_b", [P, E])
        ident_f = sb("ident_f", [P, P])
        ident_r = sb("ident_r", [P, P], F32R)
        ident_h = sb("ident_h", [P, P], BF16)
        rank = sb("rank", [P, E])
        neg_half = sb("neg_half", [P, BT])

        stats = sb("stats", [P, BT, 6])
        meanvar = sb("meanvar", [P, BT, 2])
        var_eps = sb("var_eps", [P, BT])
        rstd = sb("rstd", [P, BT])
        xn = sb("xn", [P, BT, D])
        xz = sb("xz", [P, BT, D])
        xt_f = sb("xt_f", [P, BLK])
        xt_hi = sb("xt_hi", [P, 2, BLK], BF16)
        xt_lo = sb("xt_lo", [P, 2, BLK], BF16)
        h_f = sb("h_f", [P, HS, 2, BLK])
        h_hi = sb("h_hi", [P, HS, 2, BLK], BF16)
        h_lo = sb("h_lo", [P, HS, 2, BLK], BF16)
        logits = sb("logits", [P, BT, E])
        masked = sb("masked", [P, BT, E])
        eq = sb("eq", [P, BT, E])
        ranked = sb("ranked", [P, BT, E])
        first = sb("first", [P, BT])
        top0 = sb("top0", [P, BT])
        top1 = sb("top1", [P, BT])
        hot0 = sb("hot0", [P, BT, E])
        hot1 = sb("hot1", [P, BT, E])
        gap = sb("gap", [P, BT])
        tanh_gap = sb("tanh_gap", [P, BT])
        half_w0 = sb("half_w0", [P, BT])
        half_w1 = sb("half_w1", [P, BT])
        part0 = sb("part0", [P, BT, E])
        part1 = sb("part1", [P, BT, E])
        w_tok = sb("w_tok", [P, BT, E])
        w_zero = sb("w_zero", [P, BT])

        wstage = sb("wstage", [P, 4, P])
        wq_s = sb("wq_s", [P, P])
        wq_hi = sb("wq_hi", [P, H, 32], BF16)
        wq_lo = sb("wq_lo", [P, H, 32], BF16)
        wk_hi = sb("wk_hi", [P, H, 32], BF16)
        wk_lo = sb("wk_lo", [P, H, 32], BF16)
        wv_hi = sb("wv_hi", [P, P], BF16)
        wv_lo = sb("wv_lo", [P, P], BF16)
        wo_hi = sb("wo_hi", [P, P], BF16)
        wo_lo = sb("wo_lo", [P, P], BF16)
        bstage = sb("bstage", [1, 2, P])
        bias_f = sb("bias_f", [1, 2, H, 32])
        bias_col = sb("bias_col", [P, 2, G])
        bias_sel = sb("bias_sel", [P, 2, G])
        neg_lo = sb("neg_lo", [P, 2])
        bv_b = sb("bv_b", [P, D])
        bo_b = sb("bo_b", [P, D])
        lam_b = sb("lam_b", [P, 1])
        prior_f = sb("prior_f", [P, KT, L])
        prior_hi = sb("prior_hi", [P, KT, L], F32R)
        prior_lo = sb("prior_lo", [P, KT, L], F32R)

        a_stats = sb("a_stats", [P, KT, 6])
        a_meanvar = sb("a_meanvar", [P, KT, 2])
        a_var_eps = sb("a_var_eps", [P, KT])
        a_rstd = sb("a_rstd", [P, KT])
        a_xn = sb("a_xn", [P, KT, D])
        a_xt_hi = sb("a_xt_hi", [P, L], BF16)
        a_xt_lo = sb("a_xt_lo", [P, L], BF16)
        q_op = sb("q_op", [P, 2, G, L], BF16)
        k_op = sb("k_op", [P, 2, G, L], BF16)
        q_sel = sb("q_sel", [P, 2, 2 * L], BF16)
        k_sel = sb("k_sel", [P, 2, 2 * L], BF16)
        v_op = sb("v_op", [P, 2, KT, H, 32])
        dump = sb("dump", [P, 4, L], BF16)
        row_max = sb("row_max", [P, 2, 2, KT, J])
        max_cols = sb("max_cols", [P, 2, 2, KT, J, 32], BF16)
        probs = sb("probs", [P, 2, J, 2 * L])
        ot_sb = sb("ot_sb", [P, G, L])
        rden = sb("rden", [P, KT, H])
        o_n = sb("o_n", [P, KT, D])
        o_hi = sb("o_hi", [P, L], BF16)
        o_lo = sb("o_lo", [P, L], BF16)
        o_b = sb("o_b", [P, KT, D])

        banks = ctx.enter_context(nc.psum_tensor("banks", [P, 8, 512], F32))

        x0_in, x1_in, x2_in = sem("x0_in"), sem("x1_in"), sem("x2_in")
        consts_in, w1_in, w2_in, gate_in, attn_in = (
            sem("consts_in"), sem("w1_in"), sem("w2_in"), sem("gate_in"), sem("attn_in"))
        out_stored = sem("out_stored")
        pool_set, dve_set, pool_split, ffn_ready, attn_ready, attn_pool_ready, bias_turned, bias_ready = (
            sem("pool_set"), sem("dve_set"), sem("pool_split"), sem("ffn_ready"), sem("attn_ready"),
            sem("attn_pool_ready"), sem("bias_turned"), sem("bias_ready"))
        attn_done = sem("attn_done")
        waits_met = sem("waits_met")

        def ffn_sems(k):
            names = ("stats_done var_ready rstd_ready rstd_step norm_step xn_ready xn_turned xtf_ready xt_step "
                     "xt_ready up_done h_ready lo_dve lo_pool down_done y_added gate_done "
                     "logits_read route_step gap_ready tanh_ready weight_step zero_step zero_added").split()
            return {n: sem(f"f{k}_{n}") for n in names}

        F = [ffn_sems(1), ffn_sems(2)]
        A = {n: sem(f"a_{n}") for n in (
            "stats_done var_ready rstd_ready rstd_step norm_step xn_ready xn_turned xt_hi_ready xt_ready "
            "k_done k_sel_ready k_ready q_done q_sel_ready q_ready v_done v_ready "
            "raw_done max_done max_step cols_ready cols_turned shift_ready "
            "st_done exp_done pv_done ot_ready ot_turned rden_step o_ready "
            "on_turned o_hi_ready o_ready2 proj_done biased x_added").split()}

        def tile_cols(t, n=1):
            return x_all[:, bass.ds(t * D, n * D)]

        block = ctx.enter_context(nc.Block())

        @block.sync
        def _(sp):
            x_tiles = x.rearrange("(n p) d -> p n d", p=P)
            xv = x_all[:].rearrange("p (n d) -> p n d", d=D)
            sp.dma_start(xv[:, 0:BT, :], x_tiles[:, 0:BT, :]).then_inc(x0_in, 16)
            sp.dma_start(ident_f[:], ident).then_inc(consts_in, 16)
            sp.dma_start(gate_t[:], gate).then_inc(gate_in, 16)
            sp.dma_start(ebias_b[:], ebias.broadcast_to([P, E])).then_inc(gate_in, 16)
            sp.dma_start(w1_f[:], w1).then_inc(w1_in, 16)
            sp.dma_start(w2_f[:], w2).then_inc(w2_in, 16)
            sp.dma_start(xv[:, BT:4 * BT, :], x_tiles[:, BT:4 * BT, :]).then_inc(x1_in, 16)
            for n, w in enumerate((wq, wk, wv, wo)):
                sp.dma_start(wstage[:, n, :], w).then_inc(attn_in, 16)
            sp.dma_start(bstage[:, 0, :], bq).then_inc(attn_in, 16)
            sp.dma_start(bstage[:, 1, :], bk).then_inc(attn_in, 16)
            sp.dma_start(bv_b[:], bv.broadcast_to([P, D])).then_inc(attn_in, 16)
            sp.dma_start(bo_b[:], bo.broadcast_to([P, D])).then_inc(attn_in, 16)
            sp.dma_start(lam_b[:], lam.broadcast_to([P, 1])).then_inc(attn_in, 16)
            sp.dma_start(prior_f[:], prior.rearrange("(t p) c -> p t c", p=P)).then_inc(attn_in, 16)
            sp.dma_start(xv[:, 4 * BT:TILES, :], x_tiles[:, 4 * BT:TILES, :]).then_inc(x2_in, 16)
            out_tiles = out.rearrange("(n p) d -> p n d", p=P)
            with sp.Fori(0, NB) as b:
                sp.wait_ge(F[1]["zero_added"], b + 1)
                sp.dma_start(out_tiles[:, bass.ds(b * BT, BT), :],
                             xv[:, bass.ds(b * BT, BT), :]).then_inc(out_stored, 16)
            sp.wait_ge(out_stored, 16 * NB)

        @block.tensor
        def _(pe):
            U, Y, TX, GL = (0, 1, 2, 3), (4, 5), 6, 7

            def ffn_look_ahead(S, b):
                wait(pe, S["xn_ready"], b + 1)
                wait(pe, S["xtf_ready"], b)
                for t in range(BT):
                    mm = pe.transpose(banks[:, TX, bass.ts(t, P)], xn[:, t, :], ident_f[:])
                mm.then_inc(S["xn_turned"], 1)

            def ffn_logits(S, b):
                wait(pe, S["xtf_ready"], b + 1)
                wait(pe, S["logits_read"], b)
                for t in range(BT):
                    mm = pe.matmul(banks[:, GL, bass.ts(t, E)], xt_f[:, bass.ts(t, P)], gate_t[:],
                                   start=True, stop=True)
                mm.then_inc(S["gate_done"], 1)

            def ffn_up(S, b, e, par):
                for half in range(2):
                    c = 2 * e + half
                    wait(pe, S["h_ready"], 2 * FE * b + c - 3)
                    o = banks[:, U[c % 4], :]
                    pe.matmul(o, w1_hi[:, c, :], xt_hi[:, par, :], start=True, stop=False)
                    pe.matmul(o, w1_hi[:, c, :], xt_lo[:, par, :], start=False, stop=False)
                    pe.matmul(o, w1_lo[:, c, :], xt_hi[:, par, :], start=False,
                              stop=True).then_inc(S["up_done"], 1)

            def ffn_down(S, b, e):
                m = FE * b + e
                wait(pe, S["h_ready"], 2 * m + 2)
                wait(pe, S["lo_pool"], m + 1)
                wait(pe, S["lo_dve"], m + 1)
                wait(pe, S["y_added"], m - 1)
                for t in range(BT):
                    o = banks[:, Y[e % 2], bass.ts(t, P)]
                    for half in range(2):
                        c = 2 * e + half
                        hi, lo = h_hi[:, e % HS, half, bass.ts(t, P)], h_lo[:, e % HS, half, bass.ts(t, P)]
                        pe.matmul(o, hi, w2_hi[:, c, :], start=half == 0, stop=False)
                        pe.matmul(o, hi, w2_lo[:, c, :], start=False, stop=False)
                        mm = pe.matmul(o, lo, w2_hi[:, c, :], start=False, stop=half == 1)
                mm.then_inc(S["down_done"], 1)

            def ffn_turn(S, b, par, before=True):
                wait(pe, S["xt_ready"], b + 1)
                for e in range(FE):
                    ffn_up(S, b, e, par)
                    if e == 5:
                        ffn_look_ahead(S, b + 1)
                    if e == LAG and not before:
                        pe.wait_ge(ffn_ready, 2)
                    if e >= LAG:
                        ffn_down(S, b, e - LAG)
                    elif before:
                        ffn_down(S, b - 1, FE + e - LAG)
                    if e == 7:
                        ffn_logits(S, b + 1)

            def ffn(S):
                ffn_look_ahead(S, 0)
                ffn_logits(S, 0)
                pe.wait_ge(ffn_ready, 1)
                ffn_turn(S, 0, 0, before=False)
                with pe.Fori(0, NB // 2 - 1) as i:
                    ffn_turn(S, 2 * i + 1, 1)
                    ffn_turn(S, 2 * i + 2, 0)
                ffn_turn(S, NB - 1, 1)
                for e in range(FE - LAG, FE):
                    ffn_down(S, NB - 1, e)

            pe.wait_ge(consts_in, 16)
            pe.wait_ge(gate_in, 32)
            ffn(F[0])

            ST, MX, PV, M = (0, 1), (2, 3), (4, 5), (6, 7)
            pe.wait_ge(attn_ready, 1)
            pe.wait_ge(attn_pool_ready, 1)
            pe.wait_ge(F[0]["y_added"], FE * NB)
            for which in range(2):
                for g in range(G):
                    mm = pe.matmul(banks[:, M[1], G * which + g:G * which + g + 1],
                                   bias_f[:, which, J * g:J * g + J, :].rearrange("p j c -> p (j c)"),
                                   ident_f[0:1, 0:1], start=True, stop=True)
            mm.then_inc(bias_turned, 1)
            pe.wait_ge(bias_ready, 1)

            def project(o, w_hi, w_lo, g2, done):
                for k in range(2):
                    g = 2 * g2 + k
                    cols = o[:, bass.ts(k, L)]
                    wh = w_hi[:, J * g:J * g + J, :].rearrange("p j c -> p (j c)")
                    wl = w_lo[:, J * g:J * g + J, :].rearrange("p j c -> p (j c)")
                    pe.matmul(cols, wh, a_xt_hi[:], start=True, stop=False)
                    pe.matmul(cols, wh, a_xt_lo[:], start=False, stop=False)
                    mm = pe.matmul(cols, wl, a_xt_hi[:], start=False, stop=True)
                mm.then_inc(done, 1)

            def raw_scores(b, par, v):
                gp, qt, j = v // 8, v % 8 // 4, v % 4
                wait(pe, A["q_ready"], 2 * b + gp + 1)
                wait(pe, A["k_ready"], 2 * b + gp + 1)
                wait(pe, A["max_done"], 16 * b + v - 1)
                for k in range(2):
                    r, g = 32 * j, 2 * gp + k
                    mm = pe.matmul(banks[:, MX[v % 2], bass.ts(k, L)],
                                   q_op[r:r + 32, par, g, bass.ts(qt, P)], k_op[r:r + 32, par, g, :],
                                   start=True, stop=True)
                mm.then_inc(A["raw_done"], 1)

            def scores(b, par, u):
                gp, kt, j = u // 8, u % 8 // 4, u % 4
                wait(pe, A["shift_ready"], 2 * b + gp + 1)
                wait(pe, A["exp_done"], 16 * b + u - 1)
                o = banks[:, ST[u % 2], :]
                o = banks[:, ST[u % 2], :].rearrange("p (k c) -> p k c", k=2)
                for k in range(2):
                    r, g = 32 * j, 2 * gp + k
                    pe.matmul(o[:, k, :], k_op[r:r + 32, par, g, bass.ts(kt, P)], q_op[r:r + 32, par, g, :],
                              start=k == 0, stop=True, skip_group_check=True)
                c0, c1 = max(0, kt * P - reach), min(L, kt * P + P + reach)
                pe.matmul(o[:, :, c0:c1], ident_r[:], bc(prior_hi[:, kt, c0:c1], 1, 2),
                          start=False, stop=True, skip_group_check=True)
                mm = pe.matmul(o[:, :, c0:c1], ident_r[:], bc(prior_lo[:, kt, c0:c1], 1, 2),
                               start=False, stop=True, skip_group_check=True)
                mm.then_inc(A["st_done"], 1)

            def weighted(b, par, w):
                gp, kt, k = w // 4, w % 4 // 2, w % 2
                wait(pe, A["exp_done"], 16 * b + 4 * (w // 2) + 4)
                if w == 0:
                    wait(pe, A["v_ready"], b + 1)
                    wait(pe, A["ot_ready"], 2 * b - 1)
                if w == 4:
                    wait(pe, A["ot_ready"], 2 * b)
                for j in range(J):
                    mm = pe.matmul(banks[32 * j:32 * j + 32, PV[gp], bass.ts(k, L)],
                                   v_op[:, par, kt, J * (2 * gp + k) + j, :],
                                   probs[:, w // 2 % 2, j, bass.ts(k, L)],
                                   start=kt == 0 and k == 0, stop=kt == 1, skip_group_check=True)
                mm.then_inc(A["pv_done"], 1)

            def turn_cols(b, par, gp):
                wait(pe, A["cols_ready"], 2 * b + gp + 1)
                o = banks[:, M[gp], :].bitcast(BF16)
                for k in range(2):
                    for qt in range(KT):
                        mm = pe.transpose(o[:, bass.ts(2 * k + qt, P)],
                                          max_cols[:, gp, k, qt].rearrange("p j c -> p (j c)"), ident_h[:])
                mm.then_inc(A["cols_turned"], 1)

            def turn(b, par, ahead=True, main=True, behind=True):
                nxt = 1 - par
                for u in range(16):
                    if main:
                        scores(b, par, u)
                    if u < 4 and main:
                        raw_scores(b, par, 12 + u)
                    if u >= 4 and ahead:
                        raw_scores(b + 1, nxt, u - 4)
                    if u in (5, 6, 9, 10, 13, 14) and main:
                        weighted(b, par, 2 * ((u - 5) // 4) + (u - 5) % 4)
                    if u in (1, 2) and behind:
                        weighted(b - 1, nxt, 5 + u)
                    if u == 0 and ahead:
                        wait(pe, A["xn_ready"], b + 2)
                        wait(pe, A["shift_ready"], 2 * b + 1)
                        for t in range(KT):
                            mm = pe.transpose(banks[:, M[0], bass.ts(t, P)], a_xn[:, t, :], ident_f[:])
                        mm.then_inc(A["xn_turned"], 1)
                    if u == 1 and ahead:
                        wait(pe, A["xt_ready"], b + 2)
                        project(banks[:, M[0], :], wk_hi, wk_lo, 0, A["k_done"])
                    if u == 2 and ahead:
                        wait(pe, A["q_ready"], 2 * b + 2)
                        wait(pe, A["o_ready2"], b - 1)
                        project(banks[:, M[1], :], wk_hi, wk_lo, 1, A["k_done"])
                        wait(pe, A["k_ready"], 2 * b + 3)
                        project(banks[:, M[0], :], wq_hi, wq_lo, 0, A["q_done"])
                    if u == 3 and ahead:
                        wait(pe, A["k_ready"], 2 * b + 4)
                        project(banks[:, M[1], :], wq_hi, wq_lo, 1, A["q_done"])
                    if u == 4 and ahead:
                        wait(pe, A["q_ready"], 2 * b + 3)
                        for t in range(KT):
                            o = banks[:, M[0], bass.ts(t, P)]
                            pe.matmul(o, a_xt_hi[:, bass.ts(t, P)], wv_hi[:], start=True, stop=False)
                            pe.matmul(o, a_xt_hi[:, bass.ts(t, P)], wv_lo[:], start=False, stop=False)
                            mm = pe.matmul(o, a_xt_lo[:, bass.ts(t, P)], wv_hi[:], start=False, stop=True)
                        mm.then_inc(A["v_done"], 1)
                    if u == 5 and main:
                        if ahead:
                            wait(pe, A["q_ready"], 2 * b + 4)
                        wait(pe, A["o_ready2"], b - 1)
                        turn_cols(b, par, 1)
                    if u in (6, 7) and behind:
                        qt = u - 6
                        wait(pe, A["ot_ready"], 2 * b)
                        if qt == 0:
                            wait(pe, A["v_ready"], b + 2 if ahead else NBATCH)
                            wait(pe, A["biased"], b - 1)
                        if qt == 1:
                            wait(pe, A["shift_ready"], 2 * b + 2 if main else 2 * b)
                            wait(pe, A["o_ready2"], b - 1)
                        for g in range(G):
                            mm = pe.transpose(banks[:, M[qt], bass.ts(g, P)],
                                              ot_sb[:, g, bass.ts(qt, P)], ident_f[:])
                        mm.then_inc(A["ot_turned"], 1)
                    if u == 9 and behind:
                        wait(pe, A["o_ready"], 2 * b)
                        for t in range(KT):
                            mm = pe.transpose(banks[:, M[1], bass.ts(t, P)], o_n[:, t, :], ident_f[:])
                        mm.then_inc(A["on_turned"], 1)
                    if u == 11 and behind:
                        wait(pe, A["o_ready2"], b)
                        for t in range(KT):
                            o = banks[:, M[0], bass.ts(t, P)]
                            pe.matmul(o, o_hi[:, bass.ts(t, P)], wo_hi[:], start=True, stop=False)
                            pe.matmul(o, o_hi[:, bass.ts(t, P)], wo_lo[:], start=False, stop=False)
                            mm = pe.matmul(o, o_lo[:, bass.ts(t, P)], wo_hi[:], start=False, stop=True)
                        mm.then_inc(A["proj_done"], 1)
                    if u == 13 and ahead:
                        if behind:
                            wait(pe, A["biased"], b)
                        wait(pe, A["v_ready"], b + 2)
                        turn_cols(b + 1, nxt, 0)

            turn(-1, 1, main=False, behind=False)
            turn(0, 0, behind=False)
            turn(1, 1)
            turn(2, 0)
            with pe.Fori(1, NBATCH // 2 - 1) as i:
                turn(2 * i + 1, 1)
                turn(2 * i + 2, 0)
            turn(NBATCH - 1, 1, ahead=False)
            turn(NBATCH, 0, ahead=False, main=False)

            pe.wait_ge(attn_done, 1)
            ffn(F[1])

        @block.scalar
        def _(act):
            U, TX = (0, 1, 2, 3), 6

            def ffn_xt(S, b):
                wait(act, S["xn_turned"], b + 1)
                wait(act, S["gate_done"], b)
                wait(act, S["xt_ready"], b)
                act.activation(xt_f[:], banks[:, TX, :], ACT.Copy).then_inc(S["xtf_ready"], 1)

            def ffn_tanh(S, b):
                wait(act, S["gap_ready"], b + 1)
                wait(act, S["weight_step"], 5 * b)
                act.activation(tanh_gap[:], gap[:], ACT.Tanh, scale=0.5).then_inc(S["tanh_ready"], 1)

            def ffn_turn(S, b):
                for e in range(FE):
                    m = FE * b + e
                    if e == 1:
                        ffn_tanh(S, b)
                    for half in range(2):
                        c = 2 * e + half
                        wait(act, S["up_done"], 2 * FE * b + c + 1)
                        wait(act, S["lo_pool" if half == 0 else "lo_dve"], m + 1 - HS)
                        act.activation(h_f[:, e % HS, half, :], banks[:, U[c % 4], :], ACT.Silu)
                        wait(act, S["down_done"], m + 1 - HS)
                        act.activation(h_hi[:, e % HS, half, :], banks[:, U[c % 4], :],
                                       ACT.Silu).then_inc(S["h_ready"], 1)
                    if e == 5:
                        ffn_xt(S, b + 1)

            def ffn(S):
                ffn_xt(S, 0)
                ffn_turn(S, 0)
                with act.Fori(1, NB) as b:
                    ffn_turn(S, b)

            ffn(F[0])

            ST, PV, M = (0, 1), (4, 5), (6, 7)
            act.wait_ge(attn_ready, 1)
            act.wait_ge(bias_ready, 1)
            act.wait_ge(F[0]["y_added"], FE * NB)

            def low_rows(sel, which, g2):
                for k in range(2):
                    g = 2 * g2 + k
                    i = act.activation(sel[:, g2, bass.ts(k, L)], banks[:, M[g2], bass.ts(k, L)], ACT.Identity,
                                       bias=bias_sel[:, which, g:g + 1], scale=neg_lo[:, which:which + 1])
                return i

            def turn(b, par, ahead=True, main=True, behind=True):
                nxt = 1 - par
                for u in range(16):
                    if main:
                        q = u // 4
                        wait(act, A["st_done"], 16 * b + u + 1)
                        wait(act, A["pv_done"], 8 * b + 2 * q - 2)
                        act.activation(probs[:, q % 2, u % 4, :], banks[:, ST[u % 2], :],
                                       ACT.Exp).then_inc(A["exp_done"], 1)
                    if u == 0 and ahead:
                        wait(act, A["xn_turned"], b + 2)
                        wait(act, A["v_done"], b + 1)
                        act.activation(a_xt_hi[:], banks[:, M[0], 0:L], ACT.Copy).then_inc(A["xt_hi_ready"], 1)
                    if u in (1, 2) and ahead:
                        n = 2 * (b + 1) + u - 1
                        wait(act, A["k_done"], n + 1)
                        wait(act, A["k_ready"], n - 1)
                        low_rows(k_sel, 1, u - 1).then_inc(A["k_sel_ready"], 1)
                    if u in (2, 3) and ahead:
                        n = 2 * (b + 1) + u - 2
                        wait(act, A["q_done"], n + 1)
                        wait(act, A["q_ready"], n - 1)
                        low_rows(q_sel, 0, u - 2).then_inc(A["q_sel_ready"], 1)
                    if u == 3 and behind:
                        wait(act, A["pv_done"], 8 * b)
                        wait(act, A["ot_turned"], 2 * b - 2)
                        act.activation(ot_sb[:, 2:4, :].rearrange("p g c -> p (g c)"),
                                       banks[:, PV[1], :], ACT.Copy).then_inc(A["ot_ready"], 1)
                    if u == 10 and behind:
                        wait(act, A["on_turned"], b)
                        wait(act, A["proj_done"], b - 1)
                        act.activation(o_hi[:], banks[:, M[1], 0:L], ACT.Copy).then_inc(A["o_hi_ready"], 1)
                    if u == 11 and main:
                        wait(act, A["pv_done"], 8 * b + 4)
                        wait(act, A["ot_turned"], 2 * b)
                        act.activation(ot_sb[:, 0:2, :].rearrange("p g c -> p (g c)"),
                                       banks[:, PV[0], :], ACT.Copy).then_inc(A["ot_ready"], 1)

            turn(-1, 1, main=False, behind=False)
            turn(0, 0, behind=False)
            turn(1, 1)
            turn(2, 0)
            with act.Fori(1, NBATCH // 2 - 1) as i:
                turn(2 * i + 1, 1)
                turn(2 * i + 2, 0)
            turn(NBATCH - 1, 1, ahead=False)
            turn(NBATCH, 0, ahead=False, main=False)

            act.wait_ge(attn_done, 1)
            ffn(F[1])

        @block.gpsimd
        def _(pool):
            pool.memset(x_all[:, TILES * D:], 0.0)
            pool.memset(neg_half[:], -0.5)
            pool.memset(bias_f[:], 0.0)
            pool.iota(rank[:], pattern=[[-1, E]], base=E, channel_multiplier=0,
                      allow_small_or_imprecise_dtypes=True).then_inc(pool_set, 1)
            pool.wait_ge(pool_set, 1)
            pool.memset(bias_f[:, 1, :, 3 * HD:3 * HD + 2], 1.0).then_inc(pool_set, 1)

            def attention_constants():
                n = [0]

                def done(ins):
                    n[0] += 1
                    ins.then_inc(pool_split, 1)
                    pool.wait_ge(pool_split, n[0])

                def split(hi, lo, src):
                    done(pool.tensor_copy(hi, src))
                    return pool.tensor_tensor(lo, src, hi, ALU.subtract)

                pool.memset(max_cols[:], 0.0)
                pool.memset(v_op[:], 0.0)
                pool.memset(wq_hi[:, :, 3 * HD:], 0.0)
                pool.memset(wq_lo[:, :, 3 * HD:], 0.0)
                pool.memset(wk_hi[:, :, 3 * HD:], 0.0)
                done(pool.memset(wk_lo[:, :, 3 * HD:], 0.0))
                pool.memset(v_op[:, :, :, :, HD:HD + 1], 1.0)
                pool.wait_ge(attn_in, 160)
                pool.wait_ge(dve_set, 3)
                for src, hi, lo in ((wq_s[:], wq_hi, wq_lo), (wstage[:, 1, :], wk_hi, wk_lo)):
                    s3 = src.rearrange("p (h d) -> p h d", d=HD)
                    for r in range(3):
                        split(hi[:, :, HD * r:HD * r + HD], lo[:, :, HD * r:HD * r + HD], s3)
                split(wv_hi[:], wv_lo[:], wstage[:, 2, :])
                split(wo_hi[:], wo_lo[:], wstage[:, 3, :]).then_inc(attn_pool_ready, 1)

            def root(S, b, n, ve, rs, mv):
                wait(pool, S["var_ready"], b + 1)
                alone(pool, waits_met)
                pool.tensor_scalar(ve[:], mv[:, :, 1], EPS, 1.0, ALU.add, ALU.mult).then_inc(S["rstd_step"], 1)
                wait(pool, S["rstd_step"], b + 1)
                wait(pool, S["xn_ready"], b)
                pool.tensor_tensor(rs[:], ve[:], neg_half[:, 0:n], ALU.pow).then_inc(S["rstd_ready"], 1)

            def norm_apply(S, b, tile0, n, mv, rs, dst):
                wait(pool, S["var_ready"], b + 1)
                wait(pool, S["xn_turned"], b)
                pool.tensor_tensor(dst[:], tile_cols(tile0, n).rearrange("p (t d) -> p t d", d=D),
                                   bc(mv[:, :, 0], 2, D), ALU.subtract).then_inc(S["norm_step"], 1)
                wait(pool, S["norm_step"], b + 1)
                wait(pool, S["rstd_ready"], b + 1)
                pool.tensor_tensor(dst[:], dst[:], bc(rs[:], 2, D), ALU.mult).then_inc(S["xn_ready"], 1)

            def ffn_norm(S, b):
                wait(pool, S["zero_step"], b)
                norm_apply(S, b, BT * b, BT, meanvar, rstd, xn)

            def zero_part(S, b):
                wait(pool, S["weight_step"], 5 * b + 5)
                wait(pool, S["xn_ready"], b + 1)
                wait(pool, S["zero_added"], b)
                pool.tensor_tensor(xz[:], xn[:], bc(w_zero[:], 2, D), ALU.mult).then_inc(S["zero_step"], 1)

            def zero_add(S, b):
                wait(pool, S["zero_step"], b + 1)
                wait(pool, S["y_added"], FE * (b + 1))
                xt = tile_cols(BT * b, BT)
                pool.tensor_tensor(xt, xt, xz[:].rearrange("p t d -> p (t d)"),
                                   ALU.add).then_inc(S["zero_added"], 1)

            def ffn_turn(S, b, before=True):
                for e in range(FE):
                    m = FE * b + e
                    wait(pool, S["h_ready"], 2 * m + 1)
                    wait(pool, S["down_done"], m + 1 - HS)
                    pool.tensor_tensor(h_lo[:, e % HS, 0, :], h_f[:, e % HS, 0, :], h_hi[:, e % HS, 0, :],
                                       ALU.subtract).then_inc(S["lo_pool"], 1)
                    if e == 1:
                        root(S, b + 1, BT, var_eps, rstd, meanvar)
                    if e == 2 and before:
                        zero_add(S, b - 1)
                    if e == 3:
                        zero_part(S, b)
                        ffn_norm(S, b + 1)

            def ffn(S, constants=False):
                root(S, 0, BT, var_eps, rstd, meanvar)
                ffn_norm(S, 0)
                if constants:
                    attention_constants()
                ffn_turn(S, 0, before=False)
                with pool.Fori(1, NB) as b:
                    ffn_turn(S, b)
                zero_add(S, NB - 1)

            ffn(F[0], constants=True)

            def batch_norm(b):
                root(A, b, KT, a_var_eps, a_rstd, a_meanvar)
                norm_apply(A, b, KT * b, KT, a_meanvar, a_rstd, a_xn)

            batch_norm(0)
            with pool.Fori(1, NBATCH + 1) as b:
                batch_norm(b)
            pool.wait_ge(attn_done, 1)
            ffn(F[1])

        @block.vector
        def _(dve):
            Y, TX, GL = (4, 5), 6, 7

            def norm_stats(S, b, tile0, n, st, mv):
                wait(dve, S["stats_done"], b)
                for t in range(n):
                    i = dve.bn_stats(st[:, t, :], tile_cols(tile0 + t))
                i.then_inc(S["stats_done"], 1)
                wait(dve, S["stats_done"], b + 1)
                wait(dve, S["xn_ready"], b)
                alone(dve, waits_met)
                for t in range(n):
                    i = dve.bn_aggr(mv[:, t, :], st[:, t, :])
                i.then_inc(S["var_ready"], 1)

            def link(S, b, step, ins):
                ins.then_inc(S["route_step"], 1)
                wait(dve, S["route_step"], 11 * b + step)

            def route_top(S, b):
                wait(dve, S["gate_done"], b + 1)
                wait(dve, S["weight_step"], 5 * b)
                dve.tensor_tensor(logits[:], banks[:, GL, 0:BT * E].rearrange("p (t e) -> p t e", e=E),
                                  bc(ebias_b[:], 1, BT), ALU.add).then_inc(S["logits_read"], 1)
                wait(dve, S["logits_read"], b + 1)
                link(S, b, 1, dve.tensor_reduce(top0[:], logits[:], AX.X, ALU.max))
                link(S, b, 2, dve.tensor_tensor(eq[:], logits[:], bc(top0[:], 2, E), ALU.is_equal))
                link(S, b, 3, dve.tensor_tensor(ranked[:], eq[:], bc(rank[:], 1, BT), ALU.mult))
                link(S, b, 4, dve.tensor_reduce(first[:], ranked[:], AX.X, ALU.max))
                link(S, b, 5, dve.tensor_tensor(hot0[:], bc(rank[:], 1, BT), bc(first[:], 2, E), ALU.is_equal))
                link(S, b, 6, dve.scalar_tensor_tensor(masked[:], hot0[:], LOWEST, logits[:], ALU.mult, ALU.add))
                link(S, b, 7, dve.tensor_reduce(top1[:], masked[:], AX.X, ALU.max))
                dve.tensor_tensor(gap[:], top0[:], top1[:], ALU.subtract).then_inc(S["gap_ready"], 1)

            def route_second(S, b):
                wait(dve, S["route_step"], 11 * b + 7)
                link(S, b, 8, dve.tensor_tensor(eq[:], masked[:], bc(top1[:], 2, E), ALU.is_equal))
                link(S, b, 9, dve.tensor_tensor(ranked[:], eq[:], bc(rank[:], 1, BT), ALU.mult))
                link(S, b, 10, dve.tensor_reduce(first[:], ranked[:], AX.X, ALU.max))
                dve.tensor_tensor(hot1[:], bc(rank[:], 1, BT), bc(first[:], 2, E),
                                  ALU.is_equal).then_inc(S["route_step"], 1)

            def xt_parts(S, b, nxt):
                wait(dve, S["xtf_ready"], b + 1)
                wait(dve, S["up_done"], 2 * FE * (b - 1))
                dve.tensor_copy(xt_hi[:, nxt, :], xt_f[:]).then_inc(S["xt_step"], 1)
                wait(dve, S["xt_step"], b + 1)
                dve.tensor_tensor(xt_lo[:, nxt, :], xt_f[:], xt_hi[:, nxt, :],
                                  ALU.subtract).then_inc(S["xt_ready"], 1)

            def route_weigh(S, b):
                wait(dve, S["tanh_ready"], b + 1)
                wait(dve, S["route_step"], 11 * b + 11)
                wait(dve, S["zero_step"], b)
                dve.tensor_scalar(half_w0[:], tanh_gap[:], 0.25, 0.25, ALU.mult, ALU.add)
                dve.tensor_scalar(half_w1[:], tanh_gap[:], -0.25, 0.25, ALU.mult,
                                  ALU.add).then_inc(S["weight_step"], 1)
                wait(dve, S["weight_step"], 5 * b + 1)
                dve.tensor_tensor(part0[:], hot0[:], bc(half_w0[:], 2, E), ALU.mult).then_inc(S["weight_step"], 1)
                dve.tensor_tensor(part1[:], hot1[:], bc(half_w1[:], 2, E), ALU.mult).then_inc(S["weight_step"], 1)
                wait(dve, S["weight_step"], 5 * b + 3)
                wait(dve, S["y_added"], FE * b)
                dve.tensor_tensor(w_tok[:], part0[:], part1[:], ALU.add).then_inc(S["weight_step"], 1)
                wait(dve, S["weight_step"], 5 * b + 4)
                dve.tensor_reduce(w_zero[:], w_tok[:, :, FE:E], AX.X, ALU.add).then_inc(S["weight_step"], 1)
                wait(dve, S["weight_step"], 5 * b + 5)

            def add_expert(S, b, e):
                m = FE * b + e
                wait(dve, S["down_done"], m + 1)
                wait(dve, S["y_added"], m)
                for t in range(BT):
                    xt = tile_cols(BT * b + t)
                    i = dve.scalar_tensor_tensor(xt, banks[:, Y[e % 2], bass.ts(t, P)], w_tok[:, t, e:e + 1],
                                                 xt, ALU.mult, ALU.add)
                i.then_inc(S["y_added"], 1)

            def ffn_turn(S, b, par, before=True):
                for e in range(FE):
                    m = FE * b + e
                    wait(dve, S["h_ready"], 2 * m + 2)
                    wait(dve, S["down_done"], m + 1 - HS)
                    dve.tensor_tensor(h_lo[:, e % HS, 1, :], h_f[:, e % HS, 1, :], h_hi[:, e % HS, 1, :],
                                      ALU.subtract).then_inc(S["lo_dve"], 1)
                    if e == LAG:
                        route_weigh(S, b)
                    if e >= LAG:
                        add_expert(S, b, e - LAG)
                    elif before:
                        add_expert(S, b - 1, FE + e - LAG)
                    if e == 0:
                        norm_stats(S, b + 1, BT * (b + 1), BT, stats, meanvar)
                    if e == 1:
                        route_second(S, b)
                    if e == 6:
                        xt_parts(S, b + 1, 1 - par)
                route_top(S, b + 1)

            def ffn(S, first=False):
                norm_stats(S, 0, 0, BT, stats, meanvar)
                if first:
                    first_weights()
                xt_parts(S, 0, 0)
                if first:
                    second_weights()
                route_top(S, 0)
                if first:
                    attention_constants()
                    dve.wait_ge(x1_in, 16)
                ffn_turn(S, 0, 0, before=False)
                if first:
                    dve.wait_ge(x2_in, 16)
                with dve.Fori(0, NB // 2 - 1) as i:
                    ffn_turn(S, 2 * i + 1, 1)
                    ffn_turn(S, 2 * i + 2, 0)
                ffn_turn(S, NB - 1, 1)
                for e in range(FE - LAG, FE):
                    add_expert(S, NB - 1, e)

            n = [0]

            def done(ins):
                n[0] += 1
                ins.then_inc(dve_set, 1)
                dve.wait_ge(dve_set, n[0])

            def first_weights():
                dve.wait_ge(w1_in, 16)
                w1h = w1_hi[:].rearrange("p c f -> p (c f)")
                done(dve.tensor_copy(w1h, w1_f[:]))
                dve.tensor_tensor(w1_lo[:].rearrange("p c f -> p (c f)"), w1_f[:], w1h,
                                  ALU.subtract).then_inc(ffn_ready, 1)

            def second_weights():
                dve.wait_ge(w2_in, 16)
                w2h = w2_hi[:].rearrange("p c f -> p (c f)")
                done(dve.tensor_copy(w2h, w2_f[:]))
                dve.tensor_tensor(w2_lo[:].rearrange("p c f -> p (c f)"), w2_f[:], w2h,
                                  ALU.subtract).then_inc(ffn_ready, 1)
                dve.wait_ge(attn_in, 160)
                dve.tensor_scalar(wq_s[:], wstage[:, 0, :], QSCALE, None, ALU.mult).then_inc(dve_set, 1)
                n[0] += 1

            def attention_constants():
                for r in range(3):
                    dve.tensor_scalar(bias_f[:, 0, :, HD * r:HD * r + HD],
                                      bstage[:, 0, :].rearrange("p (h d) -> p h d", d=HD), QSCALE, None, ALU.mult)
                    dve.tensor_copy(bias_f[:, 1, :, HD * r:HD * r + HD],
                                    bstage[:, 1, :].rearrange("p (h d) -> p h d", d=HD))
                dve.tensor_copy(ident_h[:], ident_f[:])
                dve.tensor_copy(ident_r[:], ident_f[:])
                iv = ident_f[:].rearrange("p (j c) -> p j c", c=32)
                dve.tensor_reduce(neg_lo[:, 0:1], iv[:, :, HD:2 * HD], AX.XY, ALU.add, negate=True)
                dve.tensor_reduce(neg_lo[:, 1:2], iv[:, :, 2 * HD:3 * HD], AX.XY, ALU.add, negate=True)
                done(dve.tensor_scalar(prior_f[:], prior_f[:], lam_b[:, 0:1], None, ALU.mult))
                done(dve.tensor_copy(prior_hi[:], prior_f[:]))
                dve.tensor_tensor(prior_lo[:], prior_f[:], prior_hi[:].bitcast(F32),
                                  ALU.subtract).then_inc(attn_ready, 1)

            dve.wait_ge(x0_in, 16)
            dve.wait_ge(consts_in, 16)
            dve.wait_ge(gate_in, 32)
            dve.wait_ge(pool_set, 2)
            ffn(F[0], first=True)

            MX, M = (2, 3), (6, 7)

            def batch_stats(b):
                norm_stats(A, b, KT * b, KT, a_stats, a_meanvar)

            def maxima(b, v):
                gp, qt, j = v // 8, v % 8 // 4, v % 4
                wait(dve, A["raw_done"], 16 * b + v + 1)
                wait(dve, A["max_done"], 16 * b + v - 1)
                if v % 8 == 0:
                    wait(dve, A["cols_ready"], 2 * b + gp - 1)
                alone(dve, waits_met)
                for k in range(2):
                    i = dve.tensor_tensor_reduce(dump[:, 2 * (v % 2) + k, :], banks[:, MX[v % 2], bass.ts(k, L)],
                                                 prior_f[:, qt, :], 1.0, LOWEST, ALU.add, ALU.max,
                                                 row_max[:, gp, k, qt, j:j + 1])
                i.then_inc(A["max_done"], 1)

            def columns(b, gp):
                wait(dve, A["max_done"], 16 * b + 8 * gp + 8)
                wait(dve, A["cols_turned"], 2 * b + gp - 1)
                rm = row_max[:, gp].rearrange("p k t j -> p (k t) j")
                mc = max_cols[:, gp].rearrange("p k t j c -> p (k t) j c")
                hi, lo = mc[:, :, :, 3 * HD], mc[:, :, :, 3 * HD + 1]
                dve.tensor_scalar(hi, rm, -1.0, None, ALU.mult).then_inc(A["max_step"], 1)
                wait(dve, A["max_step"], 2 * b + gp + 1)
                dve.scalar_tensor_tensor(lo, rm, -1.0, hi, ALU.mult, ALU.subtract).then_inc(A["cols_ready"], 1)

            def merge(b, par, gp):
                wait(dve, A["cols_turned"], 2 * b + gp + 1)
                wait(dve, A["max_done"], 16 * b + 8 * gp + 8)
                q = q_op[:, par, 2 * gp:2 * gp + 2, :].rearrange("p g c -> p (g c)")
                dve.tensor_tensor(q, banks[:, M[gp], :].bitcast(BF16)[:, 0:2 * L], q,
                                  ALU.add).then_inc(A["shift_ready"], 1)

            def operand(kind, dst, sel, b, nxt, g2):
                which = "qk".index(kind)
                wait(dve, A[kind + "_sel_ready"], 2 * (b + 1) + g2 + 1)
                for k in range(2):
                    g = 2 * g2 + k
                    i = dve.scalar_tensor_tensor(dst[:, nxt, g, :], banks[:, M[g2], bass.ts(k, L)],
                                                 bias_col[:, which, g:g + 1], sel[:, g2, bass.ts(k, L)],
                                                 ALU.add, ALU.add)
                i.then_inc(A[kind + "_ready"], 1)

            def turn(b, par, ahead=True, main=True, behind=True):
                nxt = 1 - par
                for u in range(16):
                    if u < 4 and main:
                        maxima(b, 12 + u)
                    if u >= 4 and ahead:
                        maxima(b + 1, u - 4)
                    if u == 3 and main:
                        columns(b, 1)
                    if u == 11 and ahead:
                        columns(b + 1, 0)
                    if u == 0 and ahead:
                        wait(dve, A["xt_hi_ready"], b + 2)
                        dve.tensor_tensor(a_xt_lo[:], banks[:, M[0], 0:L], a_xt_hi[:],
                                          ALU.subtract).then_inc(A["xt_ready"], 1)
                    if u in (1, 2) and ahead:
                        operand("k", k_op, k_sel, b, nxt, u - 1)
                    if u in (2, 3) and ahead:
                        operand("q", q_op, q_sel, b, nxt, u - 2)
                    if u == 4 and ahead:
                        wait(dve, A["v_done"], b + 2)
                        for t in range(KT):
                            i = dve.tensor_tensor(v_op[:, nxt, t, :, 0:HD],
                                                  banks[:, M[0], bass.ts(t, P)].rearrange("p (h d) -> p h d", d=HD),
                                                  bv_b[:].rearrange("p (h d) -> p h d", d=HD), ALU.add)
                        i.then_inc(A["v_ready"], 1)
                    if u == 5 and main:
                        merge(b, par, 1)
                    if u in (6, 7) and behind:
                        qt = u - 6
                        wait(dve, A["ot_turned"], 2 * (b - 1) + qt + 1)
                        wait(dve, A["on_turned"], b - 1)
                        ov = banks[:, M[qt], :].rearrange("p (h c) -> p h c", c=32)
                        dve.reciprocal(rden[:, qt, :], ov[:, :, HD]).then_inc(A["rden_step"], 1)
                        wait(dve, A["rden_step"], 2 * (b - 1) + qt + 1)
                        dve.tensor_tensor(o_n[:, qt, :].rearrange("p (h d) -> p h d", d=HD), ov[:, :, 0:HD],
                                          bc(rden[:, qt, :], 2, HD), ALU.mult).then_inc(A["o_ready"], 1)
                    if u == 10 and behind:
                        wait(dve, A["o_hi_ready"], b)
                        wait(dve, A["proj_done"], b - 1)
                        dve.tensor_tensor(o_lo[:], banks[:, M[1], 0:L], o_hi[:],
                                          ALU.subtract).then_inc(A["o_ready2"], 1)
                    if u == 12 and behind:
                        wait(dve, A["proj_done"], b)
                        wait(dve, A["x_added"], b - 1)
                        for t in range(KT):
                            i = dve.tensor_tensor(o_b[:, t, :], banks[:, M[0], bass.ts(t, P)], bo_b[:], ALU.add)
                        i.then_inc(A["biased"], 1)
                        wait(dve, A["biased"], b)
                        xt = tile_cols(KT * (b - 1), KT)
                        dve.tensor_tensor(xt, xt, o_b[:].rearrange("p t d -> p (t d)"),
                                          ALU.add).then_inc(A["x_added"], 1)
                    if u == 8 and ahead:
                        batch_stats(b + 2) if not (isinstance(b, int) and b + 2 > NBATCH) else None
                    if u == 13 and ahead:
                        merge(b + 1, nxt, 0)

            dve.wait_ge(F[0]["y_added"], FE * NB)
            dve.wait_ge(bias_turned, 1)
            done(dve.tensor_copy(bias_col[:].rearrange("p w g -> p (w g)"), banks[:, M[1], 0:2 * G]))
            dve.tensor_tensor(bias_sel[:], bias_col[:], bc(neg_lo[:], 2, G), ALU.mult).then_inc(bias_ready, 1)
            dve.wait_ge(F[0]["zero_added"], NB)
            batch_stats(0)
            turn(-1, 1, main=False, behind=False)
            turn(0, 0, behind=False)
            turn(1, 1)
            turn(2, 0)
            with dve.Fori(1, NBATCH // 2 - 1) as i:
                turn(2 * i + 1, 1)
                turn(2 * i + 2, 0)
            turn(NBATCH - 1, 1, ahead=False)
            turn(NBATCH, 0, ahead=False, main=False)
            dve.wait_ge(A["x_added"], NBATCH)
            dve.wait_ge(A["biased"], NBATCH)
            dve.memset(first[:], 0.0).then_inc(attn_done, 1)

            ffn(F[1])


def kernel(**inputs):
    import numpy as np
    import concourse.bacc as bacc
    from concourse.bass_utils import run_bass_kernel_spmd

    def f32(name):
        return np.asarray(inputs[name])

    x = f32("L0_attn_x")
    B, L, D = x.shape
    w1, w2 = f32("L0_ffn_w1"), f32("L0_ffn_w2")
    FE, F, _ = w1.shape
    pos = np.arange(L, dtype=np.float32)
    dist = np.abs(pos[:, None] - pos[None, :])
    prior = np.zeros_like(dist)
    for period, weight, sigma in ((1.0, 0.8, 0.5), (30.0, 0.4, 2.0)):
        prior = prior + np.float32(weight) * np.exp(-(dist - np.float32(period)) ** 2 / np.float32(2.0 * sigma ** 2))
    arrays = {
        "x": x.reshape(B * L, D),
        "wq": f32("L0_attn_Wq").T, "bq": f32("L0_attn_bq").reshape(1, D),
        "wk": f32("L0_attn_Wk").T, "bk": f32("L0_attn_bk").reshape(1, D),
        "wv": f32("L0_attn_Wv").T, "bv": f32("L0_attn_bv").reshape(1, D),
        "wo": f32("L0_attn_Wo").T, "bo": f32("L0_attn_bo").reshape(1, D),
        "lam": f32("L0_attn_prior_lambda").reshape(1, 1),
        "gate": f32("L0_ffn_gate_w").T,
        "ebias": f32("L0_ffn_expert_bias").reshape(1, -1),
        "w1": w1.transpose(2, 0, 1).reshape(D, FE * F),
        "w2": w2.transpose(0, 2, 1).reshape(FE * F // 128, 128, D).transpose(1, 0, 2).reshape(128, -1),
        "ident": np.eye(128, dtype=np.float32),
        "prior": prior.astype(np.float32),
    }
    arrays = {k: np.ascontiguousarray(v) for k, v in arrays.items()}
    nc = bacc.Bacc("TRN2", target_bir_lowering=False, num_devices=1)
    args = [nc.dram_tensor(f"in_{k}", v.shape, mybir.dt.from_np(v.dtype), kind="ExternalInput").ap()
            for k, v in arrays.items()]
    out = nc.dram_tensor("out", (B * L, D), F32, kind="ExternalOutput").ap()
    reach = int(dist[prior != 0].max())
    build(nc, *args, out, reach)
    r = run_bass_kernel_spmd(nc, [{f"in_{k}": v for k, v in arrays.items()}], core_ids=[0])
    return r.results[0]["out"].reshape(B, L, D)
```
